# Optimizing a Trainium2 kernel written in Bass

```python
import numpy as np
import jax
import jax.numpy as jnp

def _softmax(x, axis=-1):
    return jax.nn.softmax(x, axis=axis)

def _gelu(x):
    return jax.nn.gelu(x, approximate=True)

def _silu(x):
    return jax.nn.silu(x)

def _sigmoid(x):
    return jax.nn.sigmoid(x)

def _layernorm(x, axis=-1, eps=1e-05):
    m = jnp.mean(x, axis=axis, keepdims=True)
    v = jnp.var(x, axis=axis, keepdims=True)
    return (x - m) / jnp.sqrt(v + eps)

def _scatter_add(tgt, idx, src, axis=0):
    return tgt.at[idx].add(src)

def _segment_sum(src, seg, n):
    return jax.ops.segment_sum(src, seg, n)
kernel_name = 'mk_conv_seq_d2_conv_nhwc64_r4_99efa2'

def setup_inputs(seed: int=0):
    np.random.seed(seed)
    _w = jnp.asarray

    def _rec_inputs():
        import jax
        import jax.numpy as jnp
        _gk = jax.random.key(seed)
        x = -0.0003929 + 0.9999 * jax.random.normal(jax.random.fold_in(_gk, 1), (4, 64, 64, 16), jnp.float32)
        return x
    x = _rec_inputs()

    def _L0_conv_setup():
        import jax, jax.numpy as jnp
        import numpy as np
        from jax import lax
        DIM = 16
        HID = 32
        EPS = 0.001

        def _ln(x, g, b):
            mu = jnp.mean(x, axis=-1, keepdims=True)
            var = jnp.mean(jnp.square(x - mu), axis=-1, keepdims=True)
            return (x - mu) * lax.rsqrt(var + EPS) * g + b

        def _pw(x, w, b):
            return jnp.einsum('bhwc,cd->bhwd', x, w) + b
        key = jax.random.key(seed)
        ks = jax.random.split(key, 12)
        s = lambda fi, fo: (2.0 / (fi + fo)) ** 0.5
        inp = {'x': jax.random.normal(ks[0], (4, 64, 64, DIM), dtype=jnp.float32), 'g1': jnp.ones((DIM,), jnp.float32), 'b1': jnp.zeros((DIM,), jnp.float32), 'g2': jnp.ones((DIM,), jnp.float32), 'b2': jnp.zeros((DIM,), jnp.float32), 'w_te': jax.random.normal(ks[1], (DIM, HID), jnp.float32) * s(DIM, HID), 'b_te': jnp.zeros((HID,), jnp.float32), 'w_fc': jax.random.normal(ks[2], (2 * HID, 2 * HID), jnp.float32) * s(2 * HID, 2 * HID), 'b_fc': jnp.zeros((2 * HID,), jnp.float32), 'w_tp': jax.random.normal(ks[3], (HID, DIM), jnp.float32) * s(HID, DIM), 'b_tp': jnp.zeros((DIM,), jnp.float32), 'w_fe': jax.random.normal(ks[4], (DIM, HID), jnp.float32) * s(DIM, HID), 'b_fe': jnp.zeros((HID,), jnp.float32), 'w_dw': jax.random.normal(ks[5], (3, 3, 1, HID), jnp.float32) * 0.1, 'b_dw': jnp.zeros((HID,), jnp.float32), 'w_fp': jax.random.normal(ks[6], (HID, DIM), jnp.float32) * s(HID, DIM), 'b_fp': jnp.zeros((DIM,), jnp.float32)}
        return inp
    _L0_conv_all = _L0_conv_setup()
    _L0_conv_in = {k: v for k, v in _L0_conv_all.items() if k in ('g1', 'b1', 'g2', 'b2', 'w_te', 'b_te', 'w_fc', 'b_fc', 'w_tp', 'b_tp', 'w_fe', 'b_fe', 'w_dw', 'b_dw', 'w_fp', 'b_fp')}
    del _L0_conv_all

    def _L1_conv_setup():
        import jax, jax.numpy as jnp
        import numpy as np
        from jax import lax
        HEADS = 2
        PATCH = 8
        DIM = 16
        HID = DIM * 6 * HEADS
        EPS = 1e-06

        def layernorm(x, scale, bias):
            m = jnp.mean(x, axis=-1, keepdims=True)
            v = jnp.var(x, axis=-1, keepdims=True)
            return (x - m) * lax.rsqrt(v + EPS) * scale + bias

        def x_to_patch(x, heads, p):
            n, H, W, C = x.shape
            c, h, w = (C // heads, H // p, W // p)
            x = x.reshape(n, h, p, w, p, c, heads)
            return x.transpose(0, 6, 5, 1, 3, 2, 4)

        def patch_to_x(xp):
            n, heads, c, h, w, p1, p2 = xp.shape
            x = xp.transpose(0, 3, 5, 4, 6, 2, 1)
            return x.reshape(n, h * p1, w * p2, c * heads)
        key = jax.random.key(seed)
        ks = jax.random.split(key, 8)
        x = jax.random.normal(ks[0], (1, 48, 48, DIM), jnp.float32)
        w_hidden = jax.random.normal(ks[1], (DIM, HID), jnp.float32) / np.sqrt(DIM)
        w_qkv = jax.random.normal(ks[2], (3, 3, HID, HID), jnp.float32) / np.sqrt(9 * HID)
        w_out = jax.random.normal(ks[3], (2 * DIM * HEADS, DIM), jnp.float32) / np.sqrt(2 * DIM * HEADS)
        ln1_scale = 1.0 + 0.02 * jax.random.normal(ks[4], (DIM,), jnp.float32)
        ln1_bias = 0.02 * jax.random.normal(ks[5], (DIM,), jnp.float32)
        ln2_scale = 1.0 + 0.02 * jax.random.normal(ks[6], (2 * DIM * HEADS,), jnp.float32)
        ln2_bias = 0.02 * jax.random.normal(ks[7], (2 * DIM * HEADS,), jnp.float32)
        return {'x': x, 'w_hidden': w_hidden, 'w_qkv': w_qkv, 'w_out': w_out, 'ln1_scale': ln1_scale, 'ln1_bias': ln1_bias, 'ln2_scale': ln2_scale, 'ln2_bias': ln2_bias}
    _L1_conv_all = _L1_conv_setup()
    _L1_conv_in = {k: v for k, v in _L1_conv_all.items() if k in ('w_hidden', 'w_qkv', 'w_out', 'ln1_scale', 'ln1_bias', 'ln2_scale', 'ln2_bias')}
    del _L1_conv_all
    return {'x': x, 'L0_conv_g1': _L0_conv_in['g1'], 'L0_conv_b1': _L0_conv_in['b1'], 'L0_conv_g2': _L0_conv_in['g2'], 'L0_conv_b2': _L0_conv_in['b2'], 'L0_conv_w_te': _L0_conv_in['w_te'], 'L0_conv_b_te': _L0_conv_in['b_te'], 'L0_conv_w_fc': _L0_conv_in['w_fc'], 'L0_conv_b_fc': _L0_conv_in['b_fc'], 'L0_conv_w_tp': _L0_conv_in['w_tp'], 'L0_conv_b_tp': _L0_conv_in['b_tp'], 'L0_conv_w_fe': _L0_conv_in['w_fe'], 'L0_conv_b_fe': _L0_conv_in['b_fe'], 'L0_conv_w_dw': _L0_conv_in['w_dw'], 'L0_conv_b_dw': _L0_conv_in['b_dw'], 'L0_conv_w_fp': _L0_conv_in['w_fp'], 'L0_conv_b_fp': _L0_conv_in['b_fp'], 'L1_conv_w_hidden': _L1_conv_in['w_hidden'], 'L1_conv_w_qkv': _L1_conv_in['w_qkv'], 'L1_conv_w_out': _L1_conv_in['w_out'], 'L1_conv_ln1_scale': _L1_conv_in['ln1_scale'], 'L1_conv_ln1_bias': _L1_conv_in['ln1_bias'], 'L1_conv_ln2_scale': _L1_conv_in['ln2_scale'], 'L1_conv_ln2_bias': _L1_conv_in['ln2_bias']}

def reference(x, L0_conv_g1, L0_conv_b1, L0_conv_g2, L0_conv_b2, L0_conv_w_te, L0_conv_b_te, L0_conv_w_fc, L0_conv_b_fc, L0_conv_w_tp, L0_conv_b_tp, L0_conv_w_fe, L0_conv_b_fe, L0_conv_w_dw, L0_conv_b_dw, L0_conv_w_fp, L0_conv_b_fp, L1_conv_w_hidden, L1_conv_w_qkv, L1_conv_w_out, L1_conv_ln1_scale, L1_conv_ln1_bias, L1_conv_ln2_scale, L1_conv_ln2_bias):
    import jax
    import jax.numpy as jnp

    def _L0_conv_ref(x, g1, b1, g2, b2, w_te, b_te, w_fc, b_fc, w_tp, b_tp, w_fe, b_fe, w_dw, b_dw, w_fp, b_fp):
        import jax, jax.numpy as jnp
        import numpy as np
        from jax import lax
        DIM = 16
        HID = 32
        EPS = 0.001

        def _ln(x, g, b):
            mu = jnp.mean(x, axis=-1, keepdims=True)
            var = jnp.mean(jnp.square(x - mu), axis=-1, keepdims=True)
            return (x - mu) * lax.rsqrt(var + EPS) * g + b

        def _pw(x, w, b):
            return jnp.einsum('bhwc,cd->bhwd', x, w) + b
        h = _pw(_ln(x, g1, b1), w_te, b_te)
        F = jnp.fft.fft2(h.astype(jnp.complex64), axes=(1, 2))
        fr = jnp.concatenate([jnp.real(F), jnp.imag(F)], axis=-1)
        fc = jax.nn.gelu(_pw(fr, w_fc, b_fc), approximate=False)
        re, im = (fc[..., :HID], fc[..., HID:])
        sp = jnp.real(jnp.fft.ifft2(re + 1j * im, axes=(1, 2)))
        x1 = x + _pw(sp, w_tp, b_tp)
        h2 = _pw(_ln(x1, g2, b2), w_fe, b_fe)
        d = lax.conv_general_dilated(h2, w_dw, window_strides=(1, 1), padding='SAME', dimension_numbers=('NHWC', 'HWIO', 'NHWC'), feature_group_count=HID) + b_dw
        d = jax.nn.gelu(d, approximate=False)
        return x1 + _pw(d, w_fp, b_fp)

    def _L1_conv_ref(x, w_hidden, w_qkv, w_out, ln1_scale, ln1_bias, ln2_scale, ln2_bias):
        import jax, jax.numpy as jnp
        import numpy as np
        from jax import lax
        HEADS = 2
        PATCH = 8
        DIM = 16
        HID = DIM * 6 * HEADS
        EPS = 1e-06

        def layernorm(x, scale, bias):
            m = jnp.mean(x, axis=-1, keepdims=True)
            v = jnp.var(x, axis=-1, keepdims=True)
            return (x - m) * lax.rsqrt(v + EPS) * scale + bias

        def x_to_patch(x, heads, p):
            n, H, W, C = x.shape
            c, h, w = (C // heads, H // p, W // p)
            x = x.reshape(n, h, p, w, p, c, heads)
            return x.transpose(0, 6, 5, 1, 3, 2, 4)

        def patch_to_x(xp):
            n, heads, c, h, w, p1, p2 = xp.shape
            x = xp.transpose(0, 3, 5, 4, 6, 2, 1)
            return x.reshape(n, h * p1, w * p2, c * heads)
        xn = layernorm(x, ln1_scale, ln1_bias)
        hidden = jnp.einsum('nhwc,co->nhwo', xn, w_hidden)
        qkv = lax.conv_general_dilated(hidden, w_qkv, window_strides=(1, 1), padding='SAME', dimension_numbers=('NHWC', 'HWIO', 'NHWC'))
        q, k, v = jnp.split(qkv, 3, axis=-1)
        qp = x_to_patch(q, HEADS, PATCH)
        kp = x_to_patch(k, HEADS, PATCH)
        out = jnp.fft.irfft2(jnp.fft.rfft2(qp) * jnp.fft.rfft2(kp), s=(PATCH, PATCH))
        out = patch_to_x(out)
        out = layernorm(out, ln2_scale, ln2_bias)
        out = v * out
        out = jnp.einsum('nhwc,co->nhwo', out, w_out)
        return out + x

    def _gn(v, G=32, eps=1e-05):
        B_, H_, W_, C_ = v.shape
        g = v.reshape(B_, H_, W_, G, C_ // G)
        m = jnp.mean(g, axis=(1, 2, 4), keepdims=True)
        s = jnp.var(g, axis=(1, 2, 4), keepdims=True)
        return ((g - m) / jnp.sqrt(s + eps)).reshape(v.shape)

    def _ln_c(v, eps=1e-06):
        m = jnp.mean(v, axis=-1, keepdims=True)
        s = jnp.var(v, axis=-1, keepdims=True)
        return (v - m) / jnp.sqrt(s + eps)

    def _ln_t(v, eps=1e-05):
        m = jnp.mean(v, axis=-1, keepdims=True)
        s = jnp.var(v, axis=-1, keepdims=True)
        return (v - m) / jnp.sqrt(s + eps)

    def _to_tokens(v):
        B_, H_, W_, C_ = v.shape
        return v.reshape(B_, H_ * W_, C_)

    def _from_tokens(t, like):
        return t.reshape(like.shape)
    x = _L0_conv_ref(x, L0_conv_g1, L0_conv_b1, L0_conv_g2, L0_conv_b2, L0_conv_w_te, L0_conv_b_te, L0_conv_w_fc, L0_conv_b_fc, L0_conv_w_tp, L0_conv_b_tp, L0_conv_w_fe, L0_conv_b_fe, L0_conv_w_dw, L0_conv_b_dw, L0_conv_w_fp, L0_conv_b_fp)
    x = _L1_conv_ref(x, L1_conv_w_hidden, L1_conv_w_qkv, L1_conv_w_out, L1_conv_ln1_scale, L1_conv_ln1_bias, L1_conv_ln2_scale, L1_conv_ln2_bias)
    return x

_drawn_inputs = setup_inputs


def setup_inputs(seed=0):
    import zlib

    import numpy as np

    out = dict(_drawn_inputs(seed))
    spreads = {'L0_conv_g1': (1.0, 0.2),
     'L0_conv_b1': (0.0, 0.1),
     'L0_conv_g2': (1.0, 0.2),
     'L0_conv_b2': (0.0, 0.283),
     'L0_conv_b_te': (0.0, 0.1),
     'L0_conv_b_fc': (0.0, 0.8),
     'L0_conv_b_tp': (0.0, 0.1),
     'L0_conv_b_fe': (0.0, 0.1),
     'L0_conv_b_dw': (0.0, 0.1),
     'L0_conv_b_fp': (0.0, 0.1)}
    factors = {'L1_conv_ln2_scale': 3.846, 'L1_conv_ln2_bias': 4.116}
    for name, (base, spread) in spreads.items():
        noise = np.random.default_rng([zlib.crc32(name.encode()), seed]).standard_normal(out[name].shape)
        drawn = base * np.exp(spread * noise) if base else spread * noise
        out[name] = jnp.asarray(drawn.astype(out[name].dtype))
    for name, factor in factors.items():
        out[name] = (out[name] * factor).astype(out[name].dtype)
    return out
```

```python
from contextlib import ExitStack

import numpy as np
import concourse.bass as bass
from concourse import mybir

F32 = mybir.dt.float32
ACT = mybir.ActivationFunctionType
ALU = mybir.AluOpType
AX = mybir.AxisListType

P = 128
NB, S, C = 4, 64, 16
G2 = NB // 2
H0 = 32
U = S // 2 + 1
S2 = S + 2
HID = 192
CH = HID // 3
TAPS = 9
KH = TAPS * C // 2
UV = U * S
EPS0, EPS1 = 1e-3, 1e-6
NX = 4
NW = S // NX
WJ = NX + 2
KW = WJ * C + WJ
FPN = 96

CONST = {}
_at = 0
for _name, _n in (("f1c", 2 * U), ("f1s", 2 * U), ("dre", S), ("dim", S), ("mask", 2 * NB), ("selre", S), ("selim", S),
                  ("ev", 2 * S), ("e2re", P), ("e2im", P), ("ident", P), ("dq", P), ("dks", P), ("im1", P), ("im2", P),
                  ("mean", 2 * C), ("tapsel", 3 * NX * KW), ("rep", KW), ("onessel", KW)):
    CONST[_name] = (_at, _at + _n)
    _at += _n
NCONST = _at


def constants():
    k = np.zeros((P, NCONST))

    def put(name, a):
        lo, hi = CONST[name]
        k[:a.shape[0], lo:hi] = a.reshape(a.shape[0], hi - lo)

    n = np.arange(S)
    th = 2 * np.pi * np.outer(n, np.arange(U)) / S
    eye2 = np.eye(2)
    put("f1c", np.einsum("ab,yu->aybu", eye2, np.cos(th)).reshape(P, 2 * U))
    put("f1s", np.einsum("ab,yu->aybu", eye2, -np.sin(th)).reshape(P, 2 * U))
    ph = 2 * np.pi * np.outer(n, n) / S
    co, si = np.cos(ph), np.sin(ph)
    put("dre", np.concatenate([co, si]))
    put("dim", np.concatenate([-si, co]))
    mask = np.zeros((2, NB, C, 2, NB))
    for b in range(NB):
        mask[:, b, :, 0, b] = 1
        mask[0, b, :, 1, b] = 1
        mask[1, b, :, 1, b] = -1
    put("mask", mask.reshape(P, 2 * NB))
    sel = np.zeros((2, NB, 2, C, NB, C))
    for r in range(2):
        for b in range(NB):
            sel[r, b, r, :, b, :] = np.eye(C)
    put("selre", sel[0].reshape(P, S))
    put("selim", sel[1].reshape(P, S))
    put("ev", np.block([[co, si], [-si, co]]))
    w = np.zeros(S)
    w[:U] = 2
    w[0] = w[U - 1] = 1
    w = w * 0.5 / (S * S)
    put("e2re", np.kron(eye2, w[:, None] * co))
    put("e2im", np.kron(eye2, -w[:, None] * si))
    put("ident", np.eye(P))
    slots, real = [], [(0, 0), (0, 4), (4, 0), (4, 4)]
    for a in range(8):
        for b in range(8):
            if (a, b) not in real and ((-a) % 8, (-b) % 8) > (a, b):
                slots.append((a, b))
    pr, pc = np.meshgrid(np.arange(8), np.arange(8), indexing="ij")
    ang = lambda f: 2 * np.pi * (f[0] * pr + f[1] * pc).ravel() / 8
    fr, fi, i1r, i1i, i2r, i2i = (np.zeros((32, 64)) for _ in range(6))
    for s, f in enumerate(slots):
        fr[s], fi[s] = np.cos(ang(f)), -np.sin(ang(f))
        i1r[s], i1i[s] = 2 * np.cos(ang(f)) / 64, -2 * np.cos(ang(f)) / 64
        i2r[s] = i2i[s] = -2 * np.sin(ang(f)) / 64
    for s, (f, h) in enumerate(((real[0], real[1]), (real[2], real[3])), start=len(slots)):
        fr[s], fi[s] = np.cos(ang(f)), np.cos(ang(h))
        i1r[s], i1i[s] = np.cos(ang(f)) / 64, np.cos(ang(h)) / 64
    def tile(m):
        t = np.zeros((8, 2, 8, 2, 64))
        for q in range(2):
            t[:, q, :, q, :] = m.reshape(64, 8, 8).transpose(2, 1, 0)
        return t.reshape(P, P)
    put("dq", tile(np.concatenate([fr, fi])))
    put("dks", tile(np.concatenate([fi, fr])))
    put("im1", tile(np.concatenate([i1r, i1i])).T)
    put("im2", tile(np.concatenate([i2r, i2i])).T)
    put("mean", np.kron(eye2, np.full((CH, C), 1 / CH)))
    ts = np.zeros((3, 3, 3, NX, KW))
    for dy in range(3):
        for dx in range(3):
            for xx in range(NX):
                j = xx + dx
                ts[dy, dx, dy, xx, j * C:(j + 1) * C] = 1
                ts[dy, dx, dy, xx, WJ * C + j] = 1
    put("tapsel", ts.reshape(TAPS, -1))
    put("rep", np.concatenate([np.tile(np.eye(C), (1, WJ)), np.zeros((C, WJ))], 1))
    put("onessel", np.concatenate([np.zeros((C, WJ * C)), np.ones((C, WJ))], 1))
    ones = np.zeros((WJ, NW, NB, S2))
    for j in range(WJ):
        for t in range(NW):
            if 0 <= NX * t - 1 + j < S:
                ones[j, t, :, 1:S + 1] = 1
    return k.astype(np.float32), ones.reshape(WJ, -1).astype(np.float32)


def two_blocks(nc, ins, consts, ones_rows, out):
    with ExitStack() as ctx:
        def sb(name, shape):
            return ctx.enter_context(nc.sbuf_tensor(name, shape, F32))

        def sem(name):
            return ctx.enter_context(nc.semaphore(name))

        bank = [ctx.enter_context(nc.psum_tensor(f"bank{i}", [P, 512], F32)) for i in range(8)]
        padded = nc.dram_tensor("padded", (C, NB, S2, S2), F32, kind="Internal").ap()

        K = sb("K", [P, NCONST])

        def const(name, rows=P):
            lo, hi = CONST[name]
            return K[0:rows, lo:hi]

        xt = sb("xt", [P, G2, S, C])
        x1 = sb("x1", [P, G2, S, C])
        x2 = sb("x2", [P, G2, S, C])
        xc = sb("xc", [P, G2, S, C])
        sq = sb("sq", [P, G2, S, C])
        zp = sb("zp", [P, G2, S2, C])
        st = sb("st", [P, G2, 4, S])
        spec = sb("spec", [P, 2 * UV])
        f1 = spec[:, 0:UV].rearrange("p (u b c) -> p u b c", u=U, b=NB)
        hc = spec[:, UV:2 * UV]
        tr = sb("tr", [P, G2, 8, 2, S])
        UW = S * S2
        arena = sb("arena", [P, 4 * UW])
        sp = arena[:, 0:UV]
        gl = arena[:, 2176:2176 + 4096].rearrange("p (i b n) -> p i b n", i=2, b=NB)
        ht = arena[:, 6272:6272 + 4096].rearrange("p (u n) -> p u n", u=S)
        yy = arena[:, 10368:10368 + 4096].rearrange("p (j q r x) -> p j q r x", j=8, q=4, r=2)
        uw = arena[:, 0:NW * NB * S2].rearrange("p (t b y) -> p t b y", t=NW, b=NB)
        gd = arena[:, 4224:4224 + NW * NB * S].rearrange("p (t b y) -> p t b y", t=NW, b=NB)
        ui = arena[0:KH, :].rearrange("p (i h x y) -> p i h x y", i=2, h=2, x=S)

        teT = sb("teT", [H0, NB, C])
        te = sb("te", [C, H0])
        fc = sb("fc", [H0, 2, 2 * H0])
        fc2 = sb("fc2", [H0, 2, 2 * H0])
        cols = sb("cols", [P, 16])
        cte, cb1, cg1, cbfc, cg2, cb2, cbdw, cls, clb, ceps0, ceps1, chb = range(12)
        tpr = sb("tpr", [P, C])
        wmix1 = sb("wmix1", [P, NB, 2, 2 * H0])
        smix = sb("smix", [P, 2 * NB])
        wmix2 = sb("wmix2", [P, 2, C])
        fe = sb("fe", [C, H0])
        feg = sb("feg", [C, H0])
        brep = sb("brep", [C, KW])
        bfe = sb("bfe", [1, H0])
        one1 = sb("one1", [1, KW])
        dw9 = sb("dw9", [TAPS, H0])
        wfe = sb("wfe", [KW, H0])
        wdw = sb("wdw", [KW, 3, NX, H0])
        wfp = sb("wfp", [P, FPN])
        rowb = sb("rowb", [P, 4, C])
        hid = sb("hid", [C, HID])
        hidT = sb("hidT", [HID // 2, 2, C])
        wq = sb("wq", [HID // 2, 2, TAPS, HID])
        wc16 = sb("wc16", [C, TAPS, HID])
        wc = sb("wc", [KH, 2, HID])
        wor = sb("wor", [P, C])
        wo1 = sb("wo1", [P, 2, C])
        wo2 = sb("wo2", [P, 2, C])
        tile = sb("tile", [KH, 2, 2, 4, P])
        qk = sb("qk", [P, 2, 4, P])
        kh = sb("kh", [P, 2, 2, 4, CH])
        pr = sb("pr", [P, 2, 2, 4, CH])
        four = lambda a: a.rearrange("p (i k n) -> p i k n", i=2, k=4)
        vs, os_ = four(spec[:, 0:2048]), four(spec[:, UV:UV + 2048])
        oq = four(sq[:, :, :, :].rearrange("p g x c -> p (g x c)"))
        vo = four(zp[:, :, :, :].rearrange("p g x c -> p (g x c)")[:, 0:2048])
        stt = x1[:, :, :, :].rearrange("p g x c -> p (g x c)").rearrange("p (s n) -> p s n", s=8)
        ot = xt

        ld_x, ld_k, ld_w, ld_q, ld_ones, ld_wc, ld_zero, ld_wfp = map(
            sem, "ld_x ld_k ld_w ld_q ld_ones ld_wc ld_zero ld_wfp".split())
        setp, setup_pe, setup_dve, setup_pool = map(sem, "setp setup_pe setup_dve setup_pool".split())
        chain = sem("chain")
        sq_done, sd_done, z_done = sem("sq_done"), sem("sd_done"), sem("z_done")
        f1_mm, f1_dve, f1_act = sem("f1_mm"), sem("f1_dve"), sem("f1_act")
        f2_mm, f2_ev = sem("f2_mm"), sem("f2_ev")
        m1_mm, gelu1 = sem("m1_mm"), sem("gelu1")
        m2_mm, m2_ev = sem("m2_mm"), sem("m2_ev")
        ht_mm, ht_ev, ht_zero = sem("ht_mm"), sem("ht_ev"), sem("ht_zero")
        i1_mm, i1_dve, i1_act = sem("i1_mm"), sem("i1_dve"), sem("i1_act")
        i2_mm, x1_done, xb_done, x1b_done = sem("i2_mm"), sem("x1_done"), sem("xb_done"), sem("x1b_done")
        w_mm, w_dve, w_act = sem("w_mm"), sem("w_dve"), sem("w_act")
        hidt_done = sem("hidt_done")
        dw_mm, gelu2, fp_mm, x2_done = sem("dw_mm"), sem("gelu2"), sem("fp_mm"), sem("x2_done")
        xn_done, tr_mm, tr_ev, st_dma = sem("xn_done"), sem("tr_mm"), sem("tr_ev"), sem("st_dma")
        im_ld = [sem("im_ld0"), sem("im_ld1")]
        tiled, qk_mm, qk_ev, v_mm, v_ev = sem("tiled"), sem("qk_mm"), sem("qk_ev"), sem("v_mm"), sem("v_ev")
        f_mm, k_ev, prod, o_mm, o_ev, osq, vo_done = map(sem, "f_mm k_ev prod o_mm o_ev osq vo_done".split())
        r_mm, r_act, r_var, r_sd, r0_free, c_mm, ft_done, t_mm, out_add, out_st = map(
            sem, "r_mm r_act r_var r_sd r0_free c_mm ft_done t_mm out_add out_st".split())

        block = ctx.enter_context(nc.Block())
        NLW = 0

        def col(i, lo=0, hi=P):
            return cols[lo:hi, i:i + 1]

        def vec(name):
            return ins[name].rearrange("(p a) -> p a", a=1)

        def fan(v, n):
            return v.rearrange("(a n) -> a n", a=1).broadcast_to([n, v.shape[0]])

        small = [
            (te[:, :], ins["L0_conv_w_te"]),
            (fc[:, :, :], ins["L0_conv_w_fc"].rearrange("(r h) n -> h r n", r=2)),
            (fc2[:, 0, :], ins["L0_conv_w_fc"][0:H0, :]),
            (fc2[:, 1, :], ins["L0_conv_w_fc"][0:H0, :]),
            (col(cte, 0, H0), vec("L0_conv_b_te")), (col(cb1, 0, C), vec("L0_conv_b1")),
        ] + [(col(cg1, C * i, C * i + C), vec("L0_conv_g1")) for i in range(8)] + [
            (col(cbfc, 64 * i, 64 * i + 64), vec("L0_conv_b_fc")) for i in range(2)] + [
            (tpr[H0 * i:H0 * i + H0, :], ins["L0_conv_w_tp"]) for i in range(4)] + [
            (rowb[:, 0, :], fan(ins["L0_conv_b_tp"], P)), (rowb[:, 1, :], fan(ins["L0_conv_b_fp"], P)),
            (rowb[:, 2, :], fan(ins["L1_conv_ln1_scale"], P)), (rowb[:, 3, :], fan(ins["L1_conv_ln1_bias"], P)),
            (fe[:, :], ins["L0_conv_w_fe"]), (col(cg2, 0, C), vec("L0_conv_g2")), (col(cb2, 0, C), vec("L0_conv_b2")),
            (bfe[:, :], fan(ins["L0_conv_b_fe"], 1)), (dw9[:, :], ins["L0_conv_w_dw"].rearrange("a b i h -> (a b i) h")),
        ] + [(col(cbdw, H0 * i, H0 * i + H0), vec("L0_conv_b_dw")) for i in range(4)] + [
            (wor[CH * i:CH * i + CH, :], ins["L1_conv_w_out"]) for i in range(2)] + [
            (col(cls, CH * i, CH * i + CH), vec("L1_conv_ln2_scale")) for i in range(2)] + [
            (col(clb, CH * i, CH * i + CH), vec("L1_conv_ln2_bias")) for i in range(2)] + [
            (hid[:, :], ins["L1_conv_w_hidden"])]
        wfp_blocks = [(wfp[H0 * i:H0 * i + H0, C * i:C * i + C], ins["L0_conv_w_fp"]) for i in range(NX)]
        N_SMALL = 16 * (NB + len(small))

        def f1_evac(copy, j):
            g, c4 = divmod(j, 4)
            src = bank[j][:, 0:4 * 2 * U].rearrange("p (c b u) -> p c b u", c=4, b=2)
            return copy(f1[:, :, 2 * g:2 * g + 2, 4 * c4:4 * c4 + 4].rearrange("p u b c -> p c b u"), src)

        def w_evac(copy, j):
            g, t4 = divmod(j, 4)
            src = bank[j][0:WJ * C, :].rearrange("p (t b y) -> p t b y", t=4, b=2)
            return copy(uw[0:WJ * C, 4 * t4:4 * t4 + 4, 2 * g:2 * g + 2, 1:S + 1], src)

        @block.sync
        def _(sp_):
            xin = ins["x"].rearrange("(g b) y x c -> g (b y) x c", g=G2)
            for g in range(G2):
                sp_.dma_start(xt[:, g], xin[g]).then_inc(ld_x, 16)
                sp_.wait_ge(ld_x, 16 * (g + 1))
            sp_.dma_start(K[:, :], consts).then_inc(ld_k, 16)
            wqv = ins["L1_conv_w_qkv"].rearrange("ky kx (q i) o -> i q ky kx o", q=2)
            for q in range(2):
                for ky in range(3):
                    sp_.dma_start(wq[:, q, ky::3, :], wqv[:, q, ky]).then_inc(ld_q, 16)
            sp_.wait_ge(i2_mm, 4)
            sp_.dma_start(uw[WJ * C:KW, :, :, :].rearrange("p t b y -> p (t b y)"), ones_rows).then_inc(ld_ones, 16)
            sp_.wait_ge(setup_dve, 5)
            for hf in range(2):
                for t in range(TAPS):
                    sp_.dma_start(wc[8 * t:8 * t + 8, hf, :], wc16[8 * hf:8 * hf + 8, t, :]).then_inc(ld_wc, 16)
            sp_.wait_ge(ld_zero, 16)
            for b in range(NB):
                g, b2 = divmod(b, 2)
                sp_.wait_ge(tr_ev, 2 * (g + 1))
                for xx in range(8):
                    dst = padded[:, b, 1 + xx:1 + xx + 57:8, 1:S + 1]
                    sp_.dma_start(dst, tr[C * xx:C * xx + C, g, :, b2, :]).then_inc(st_dma, 16)
            for b in range(NB):
                if b == 0:
                    sp_.wait_ge(gelu2, 8)
                    sp_.wait_ge(fp_mm, 8)
                if b >= 2:
                    sp_.wait_ge(tiled, 8 * (b - 1))
                sp_.wait_ge(st_dma, 16 * 8 * NB)
                for hf in range(2):
                    for t in range(TAPS):
                        dx, dy = divmod(t, 3)
                        src = padded[8 * hf:8 * hf + 8, b].rearrange("c x y -> c (x y)")
                        n = min(UW, S2 * S2 - (dx * S2 + dy))
                        sp_.dma_start(ui[8 * t:8 * t + 8, b % 2, hf].rearrange("p x y -> p (x y)")[:, 0:n],
                                      src[:, dx * S2 + dy:dx * S2 + dy + n]).then_inc(im_ld[b % 2], 16)
            ov = out.rearrange("(g b) y x c -> g (b y) x c", g=G2)
            for u in range(8):
                g, q = divmod(u, 4)
                sp_.wait_ge(out_add, u + 1)
                sp_.dma_start(ov[g, 32 * q:32 * q + 32], ot[32 * q:32 * q + 32, g]).then_inc(out_st, 16)
            sp_.wait_ge(out_st, 16 * 8)

        @block.gpsimd
        def _(pool):
            pool.memset(wfp[:, :], 0.0).then_inc(setup_pool, 1)
            pool.memset(tr[:, :, :, :, :], 0.0).then_inc(setup_pool, 1)
            pool.memset(wmix2[:, :, :], 0.0).then_inc(setup_pool, 1)
            pool.memset(wo1[:, :, :], 0.0).then_inc(setup_pool, 1)
            pool.memset(wo2[:, :, :], 0.0).then_inc(setup_pool, 1)
            pool.memset(one1[:, 0:WJ * C], 0.0).then_inc(setup_pool, 1)
            pool.memset(one1[:, WJ * C:KW], 1.0).then_inc(setup_pool, 1)
            pool.memset(col(ceps0), EPS0).then_inc(setup_pool, 1)
            pool.memset(col(ceps1), EPS1).then_inc(setup_pool, 1)
            pool.memset(ht[:, U:S, :], 0.0).then_inc(ht_zero, 1)
            pool.wait_ge(setup_pool, 9)
            zrow = tr[:, :, :, :, :].rearrange("p g x b y -> p (g x b y)")
            flat = padded.rearrange("c b x y -> (c b x y)")
            n = C * NB * S2 * S2 // P
            pool.dma_start(flat[0:P * 2048].rearrange("(p n) -> p n", p=P), zrow[:, 0:2048]).then_inc(ld_zero, 16)
            rest = C * NB * S2 * S2 - P * 2048
            pool.wait_ge(ld_zero, 16)
            pool.dma_start(flat[P * 2048:].rearrange("(p n) -> p n", p=P), zrow[:, 0:rest // P]).then_inc(ld_zero, 16)
            for dst, src in wfp_blocks:
                pool.dma_start(dst, src).then_inc(ld_wfp, 16)
            pool.wait_ge(ld_w, N_SMALL)
            pool.wait_ge(ld_x, 32)
            pool.wait_ge(z_done, G2)
            for g in range(G2):
                pool.tensor_tensor(xt[:, g], xt[:, g], rowb[:, 0:1, :].broadcast_to([P, S, C]), ALU.add).then_inc(xb_done, 1)
            pool.memset(zp[:, :, 0:S2:S2 - 1, :], 0.0).then_inc(xb_done, 1)
            for g in range(G2):
                pool.wait_ge(z_done, G2 + g + 1)
                pool.tensor_tensor(x1[:, g], x1[:, g], rowb[:, 1:2, :].broadcast_to([P, S, C]), ALU.add).then_inc(x1b_done, 1)

        @block.scalar
        def _(act):
            with nc.allow_non_contiguous_dma(reason="w_te transposed, 512 elements, for each image"):
                for b in range(NB):
                    act.dma_start(teT[:, b, :], ins["L0_conv_w_te"].rearrange("c h -> h c")).then_inc(ld_w, 16)
            for dst, src in small:
                act.dma_start(dst, src).then_inc(ld_w, 16)

            def norm(k, eps, src):
                for g in range(G2):
                    act.wait_ge(setp, 2 * k + g + 1)
                    act.activation(sq[:, g], xc[:, g], ACT.Square).then_inc(sq_done, 1)
                for g in range(G2):
                    act.wait_ge(sd_done, 4 * k + 2 * g + 1)
                    act.activation(st[:, g, 2, :], st[:, g, 1, :], ACT.Sqrt, bias=col(eps), scale=1.0 / C).then_inc(sd_done, 1)

            act.wait_ge(setup_pool, 9)
            norm(0, ceps0, xt)
            for j in range(1, 8, 2):
                act.wait_ge(f1_mm, j + 1)
                f1_evac(act.copy, j).then_inc(f1_act, 1)
            act.wait_ge(ld_w, N_SMALL)
            for n in range(5):
                w = min(512, UV - 512 * n)
                for b in range(NB):
                    act.wait_ge(m1_mm, NB * n + b + 1)
                    if n >= 2:
                        act.wait_ge(m2_mm, n - 1)
                    act.activation(gl[:, n % 2, b, 0:w], bank[4 + b][:, 0:w], ACT.Gelu, bias=col(cbfc)).then_inc(gelu1, 1)
            for j in range(1, 8, 2):
                act.wait_ge(i1_mm, j + 1)
                act.copy(yy[:, j].rearrange("p q r x -> p (q r x)"), bank[j][:, :]).then_inc(i1_act, 1)
            norm(1, ceps0, x1)
            for j in range(1, 8, 2):
                act.wait_ge(w_mm, j + 1)
                w_evac(act.copy, j).then_inc(w_act, 1)
            act.wait_ge(w_mm, 9)
            act.copy(hidT[:, :, :].rearrange("p q c -> p (q c)"), bank[7][0:HID // 2, 0:2 * C]).then_inc(hidt_done, 1)
            for j in range(8):
                act.wait_ge(dw_mm, j + 1)
                act.activation(gd[:, 2 * j:2 * j + 2], bank[j % 4][:, :].rearrange("p (t b y) -> p t b y", t=2, b=NB),
                               ACT.Gelu, bias=col(cbdw)).then_inc(gelu2, 1)
            norm(2, ceps1, x2)

            for n in range(32 + 7):
                if n < 32:
                    u, k = divmod(n, 4)
                    act.wait_ge(v_mm, n + 1)
                    if u >= 2:
                        act.wait_ge(c_mm, u - 1)
                    act.copy(vs[:, u % 2, k, :], bank[2][:, 0:256]).then_inc(v_ev, 1)
                m = n - 1
                if 0 <= m < 32:
                    act.wait_ge(f_mm, m + 1)
                    if m >= 2:
                        act.wait_ge(prod, m - 1)
                    act.copy(kh[:, m % 2].rearrange("p s t c -> p (s t c)"), bank[4][:, :]).then_inc(k_ev, 1)
                m = n - 2
                if 0 <= m < 32:
                    u, k = divmod(m, 4)
                    act.wait_ge(o_mm, m + 1)
                    if u >= 2:
                        act.wait_ge(r_mm, u - 1)
                    act.copy(os_[:, u % 2, k, :], bank[5][:, 0:256]).then_inc(o_ev, 1)
                    act.wait_ge(o_ev, m + 1)
                    act.activation(oq[:, u % 2, k, :], os_[:, u % 2, k, :], ACT.Square).then_inc(osq, 1)
                if n >= 6 and (n - 6) % 4 == 0 and (n - 6) // 4 < 8:
                    u = (n - 6) // 4
                    act.wait_ge(r_mm, u + 1)
                    act.copy(stt[:, 0, :], bank[6][:, 0:256])
                    act.activation(stt[:, 1, :], bank[6][:, 0:256], ACT.Square).then_inc(r_act, 1)
                    act.wait_ge(r_var, u + 1)
                    act.activation(stt[:, 3, :], stt[:, 2, :], ACT.Sqrt, bias=col(ceps1)).then_inc(r_sd, 1)

        @block.vector
        def _(dve):
            done = [0]

            def link(ins_):
                ins_.then_inc(chain, 1)
                done[0] += 1
                dve.wait_ge(chain, done[0])

            def bc(a):
                return a.rearrange("p (x a) -> p x a", a=1).broadcast_to([P, S, C])

            def norm(k, src, dst, ready):
                for g in range(G2):
                    ready(g)
                    link(dve.tensor_reduce(out=st[:, g, 0, :], in_=src[:, g], axis=AX.X, op=ALU.add))
                    link(dve.tensor_scalar(st[:, g, 0, :], st[:, g, 0, :], 1.0 / C, None, ALU.mult))
                    dve.tensor_tensor(xc[:, g], src[:, g], bc(st[:, g, 0, :]), ALU.subtract).then_inc(setp, 1)
                for g in range(G2):
                    dve.wait_ge(sq_done, 2 * k + g + 1)
                    dve.tensor_reduce(out=st[:, g, 1, :], in_=sq[:, g], axis=AX.X, op=ALU.add).then_inc(sd_done, 1)
                    dve.wait_ge(sd_done, 4 * k + 2 * g + 2)
                    link(dve.reciprocal(st[:, g, 3, :], st[:, g, 2, :]))
                    dve.tensor_tensor(dst(g), xc[:, g], bc(st[:, g, 3, :]), ALU.mult).then_inc(z_done, 1)

            norm(0, xt, lambda g: sq[:, g], lambda g: dve.wait_ge(ld_x, 16 * (g + 1)))
            for j in range(0, 8, 2):
                dve.wait_ge(f1_mm, j + 1)
                f1_evac(dve.tensor_copy, j).then_inc(f1_dve, 1)

            dve.wait_ge(ld_w, N_SMALL)
            dve.wait_ge(ld_k, 16)
            dve.wait_ge(setup_pool, 9)
            dve.tensor_scalar(feg[:, :], fe[:, :], col(cg2, 0, C), None, ALU.mult)
            dve.tensor_scalar(brep[:, :], const("onessel", C), col(cb2, 0, C), None, ALU.mult).then_inc(setup_dve, 1)
            link(dve.tensor_scalar(smix[:, :], const("mask"), col(cg1), None, ALU.mult))
            dve.wait_ge(setup_pe, 1)
            for b in range(NB):
                for s in range(2):
                    dve.tensor_scalar(wmix1[:, b, s, :], bank[5][:, 0:2 * H0], smix[:, NB * s + b:NB * s + b + 1], None, ALU.mult)
            dve.tensor_scalar(cols[0:H0, chb:chb + 1], bank[5][0:H0, 64:65], col(cte, 0, H0), float(S * S), ALU.add, ALU.mult)
            for i in range(4):
                dve.tensor_scalar(wmix2[H0 * i:H0 * i + H0, i % 2, :], tpr[H0 * i:H0 * i + H0, :],
                                  -1.0 if i == 3 else 1.0, None, ALU.mult)
            for i in range(2):
                r = slice(CH * i, CH * i + CH)
                dve.tensor_scalar(wo1[r, i, :], wor[r, :], col(cls, CH * i, CH * i + CH), None, ALU.mult)
                dve.tensor_scalar(wo2[r, i, :], wor[r, :], col(clb, CH * i, CH * i + CH), None, ALU.mult).then_inc(setup_dve, 1)

            for n in range(5):
                w = min(512, UV - 512 * n)
                dve.wait_ge(f2_mm, n + 1)
                dve.tensor_copy(sp[:, 512 * n:512 * n + w], bank[n][:, 0:w]).then_inc(f2_ev, 1)
            dve.wait_ge(setup_pe, 2)
            link(dve.tensor_copy(wfe[:, :], bank[3][0:KW, 384:384 + H0]))
            dve.tensor_tensor(wdw[:, :, :, :].rearrange("p a b h -> p (a b) h"),
                              bank[3][0:KW, 0:384].rearrange("p (a h) -> p a h", h=H0),
                              wfe[:, :].rearrange("p (a h) -> p a h", a=1).broadcast_to([KW, 3 * NX, H0]),
                              ALU.mult).then_inc(setup_dve, 1)
            for n in range(6):
                if n < 5:
                    w = min(512, UV - 512 * n)
                    dve.wait_ge(m2_mm, n + 1)
                    dve.tensor_copy(hc[:, 512 * n:512 * n + w], bank[n % 2][:, 0:w]).then_inc(m2_ev, 1)
                if n >= 1:
                    m = n - 1
                    w = min(512, UV - 512 * m)
                    dve.wait_ge(ht_mm, m + 1)
                    dve.tensor_copy(ht[:, 8 * m:8 * m + w // S, :].rearrange("p u n -> p (u n)"),
                                    bank[2 + m % 2][:, 0:w]).then_inc(ht_ev, 1)
            for j in range(0, 8, 2):
                dve.wait_ge(i1_mm, j + 1)
                dve.tensor_copy(yy[:, j].rearrange("p q r x -> p (q r x)"), bank[j][:, :]).then_inc(i1_dve, 1)
            for j in range(4):
                g, c8 = divmod(j, 2)
                dve.wait_ge(i2_mm, j + 1)
                dve.wait_ge(xb_done, 2)
                dve.tensor_tensor(x1[:, g, :, 8 * c8:8 * c8 + 8].rearrange("p x c -> p c x"),
                                  bank[j][:, :].rearrange("p (c x) -> p c x", c=8),
                                  xt[:, g, :, 8 * c8:8 * c8 + 8].rearrange("p x c -> p c x"), ALU.add).then_inc(x1_done, 1)
            dve.wait_ge(xb_done, 3)
            norm(1, x1, lambda g: zp[:, g, 1:S + 1], lambda g: dve.wait_ge(x1_done, 2 * g + 2))
            dve.memset(uw[0:WJ * C, :, :, 0:S2:S2 - 1], 0.0).then_inc(w_dve, 1)
            for j in range(0, 8, 2):
                dve.wait_ge(w_mm, j + 1)
                w_evac(dve.tensor_copy, j).then_inc(w_dve, 1)
            for q in range(2):
                dve.wait_ge(setup_pe, 3 + q)
                r = [(0, 5), (5, 9)][q]
                for t in range(*r):
                    i = dve.tensor_copy(wc16[:, t, :], bank[4 + (t - r[0]) // 2][0:C, 192 * ((t - r[0]) % 2):192 * ((t - r[0]) % 2) + 192])
                if q == 0:
                    i.then_inc(setup_pool, 1)
                else:
                    i.then_inc(setup_dve, 1)
            for j in range(8):
                g, t4 = divmod(j, 4)
                dve.wait_ge(fp_mm, j + 1)
                dve.wait_ge(x1b_done, g + 1)
                dve.tensor_tensor(x2[:, g, 16 * t4:16 * t4 + 16, :].rearrange("p (t x) c -> p t (x c)", t=4),
                                  bank[4 + j % 4][:, 0:4 * FPN].rearrange("p (t n) -> p t n", t=4)[:, :, 0:NX * C],
                                  x1[:, g, 16 * t4:16 * t4 + 16, :].rearrange("p (t x) c -> p t (x c)", t=4),
                                  ALU.add).then_inc(x2_done, 1)
            norm(2, x2, lambda g: xc[:, g], lambda g: dve.wait_ge(x2_done, 4 * g + 4))
            for g in range(G2):
                dve.wait_ge(z_done, 2 * G2 + g + 1)
                link(dve.tensor_tensor(xc[:, g], xc[:, g], rowb[:, 2:3, :].broadcast_to([P, S, C]), ALU.mult))
                dve.tensor_tensor(xc[:, g], xc[:, g], rowb[:, 3:4, :].broadcast_to([P, S, C]), ALU.add).then_inc(xn_done, 1)
            for j in range(4):
                dve.wait_ge(tr_mm, j + 1)
                dve.tensor_copy(tr[:, j // 2, 4 * (j % 2):4 * (j % 2) + 4], bank[j][:, :].rearrange("p (t b y) -> p t b y", t=4, b=2)).then_inc(tr_ev, 1)

            def gather(n):
                u, k = divmod(n, 4)
                b, yh = divmod(u, 2)
                if n % 8 == 0:
                    dve.wait_ge(im_ld[b % 2], 16 * 2 * TAPS * (b // 2 + 1))
                if n >= 2:
                    dve.wait_ge(v_mm, n - 1)
                for hf in range(2):
                    src = ui[:, b % 2, hf, 16 * k:16 * k + 16, 32 * yh:32 * yh + 32].rearrange("p x (t y) -> p t x y", t=2)
                    o = dve.tensor_copy(tile[:, n % 2, hf].rearrange("p (t h) (x y) -> p t (h x) y", t=2, x=8), src)
                o.then_inc(tiled, 1)

            gather(0)
            for n in range(32 + 9):
                if n + 1 < 32:
                    gather(n + 1)
                if n < 32:
                    dve.wait_ge(qk_mm, n + 1)
                    if n >= 2:
                        dve.wait_ge(f_mm, n - 1)
                    dve.tensor_copy(qk[:, n % 2].rearrange("p t c -> p (t c)"), bank[n % 2][:, :]).then_inc(qk_ev, 1)
                m = n - 1
                if 0 <= m < 32:
                    dve.wait_ge(k_ev, m + 1)
                    if m >= 2:
                        dve.wait_ge(o_mm, m - 1)
                    qv = bank[3][:, 0:256].rearrange("p (a n) -> p a n", a=1).broadcast_to([P, 2, 256])
                    dve.tensor_tensor(pr[:, m % 2].rearrange("p s t c -> p s (t c)"), qv,
                                      kh[:, m % 2].rearrange("p s t c -> p s (t c)"), ALU.mult).then_inc(prod, 1)
                m = n - 2
                if 0 <= m < 32:
                    u, k = divmod(m, 4)
                    dve.wait_ge(o_ev, m + 1)
                    if u >= 2:
                        dve.wait_ge(r_mm, u - 1)
                    dve.tensor_tensor(vo[:, u % 2, k, :], vs[:, u % 2, k, :], os_[:, u % 2, k, :], ALU.mult).then_inc(vo_done, 1)
                if n >= 6 and (n - 6) % 4 == 0 and (n - 6) // 4 < 8:
                    u = (n - 6) // 4
                    dve.wait_ge(r_act, u + 1)
                    link(dve.tensor_tensor(stt[:, 2, :], bank[6][:, 256:512], stt[:, 1, :], ALU.subtract))
                    dve.tensor_scalar(stt[:, 2, :], stt[:, 2, :], 0.0, None, ALU.max).then_inc(r_var, 1)
                    link(dve.tensor_tensor(stt[:, 4, :], bank[7][:, 256:512], stt[:, 0, :], ALU.mult))
                    link(dve.tensor_tensor(stt[:, 4, :], bank[7][:, 0:256], stt[:, 4, :], ALU.subtract))
                    dve.wait_ge(r_sd, u + 1)
                    link(dve.reciprocal(stt[:, 5, :], stt[:, 3, :]))
                    link(dve.tensor_tensor(stt[:, 6, :], stt[:, 4, :], stt[:, 5, :], ALU.mult))
                if n >= 7 and (n - 7) % 4 == 0 and (n - 7) // 4 < 8:
                    u = (n - 7) // 4
                    dve.wait_ge(c_mm, u + 1)
                    txy = lambda a: a.rearrange("p (t x y) -> p t x y", t=2, x=8)
                    dve.tensor_tensor(stt[:, 7, :].rearrange("p (x t y) -> p t x y", t=2, x=8), txy(bank[6][:, 0:256]),
                                      txy(stt[:, 6, :]), ALU.add).then_inc(ft_done, 1)
                if n >= 8 and (n - 8) % 4 == 0 and (n - 8) // 4 < 8:
                    u = (n - 8) // 4
                    g, q = divmod(u, 4)
                    dve.wait_ge(t_mm, u + 1)
                    rows = slice(32 * q, 32 * q + 32)
                    for i in range(2):
                        res = lambda a: a[rows, g].rearrange("p (k e) c -> p k e c", k=8)[:, :, 4 * i:4 * i + 4, :]
                        o = dve.tensor_tensor(res(ot), bank[6 + i][rows, :].rearrange("p (e k c) -> p k e c", e=4, k=8),
                                              res(x2), ALU.add)
                    o.then_inc(out_add, 1)

        @block.tensor
        def _(pe):
            mm = pe.matmul
            pe.wait_ge(ld_k, 16)
            for j in range(8):
                g, c4 = divmod(j, 4)
                pe.wait_ge(z_done, g + 1)
                for c in range(4):
                    for r, name in enumerate(("f1c", "f1s")):
                        last = mm(bank[j][64 * r:64 * r + 64, 2 * U * c:2 * U * (c + 1)], sq[:, g, :, 4 * c4 + c], const(name),
                                  start=True, stop=True)
                last.then_inc(f1_mm, 1)
            pe.wait_ge(ld_w, N_SMALL)
            pe.wait_ge(f1_act, 3)
            for r in range(2):
                mm(bank[5][64 * r:64 * r + 64, 0:2 * H0], teT[:, :, :].rearrange("h b c -> h (b c)"), fc[:, r, :], start=True, stop=True)
            mm(bank[5][0:H0, 64:65], te[:, :], col(cb1, 0, C), start=True, stop=True).then_inc(setup_pe, 1)
            pe.wait_ge(f1_act, 4)
            pe.wait_ge(f1_dve, 4)
            for n in range(5):
                for u in range(8 * n, min(8 * n + 8, U)):
                    for r, name in enumerate(("dre", "dim")):
                        last = mm(bank[n][64 * r:64 * r + 64, S * (u % 8):S * (u % 8) + S],
                                  f1[:, u].rearrange("p b c -> p (b c)"), const(name), start=True, stop=True)
                last.then_inc(f2_mm, 1)

            def ht_step(m):
                pe.wait_ge(m2_ev, m + 1)
                if m >= 2:
                    pe.wait_ge(ht_ev, m - 1)
                for u in range(8 * m, min(8 * m + 8, U)):
                    for r, name in enumerate(("selre", "selim")):
                        last = mm(bank[2 + m % 2][64 * r:64 * r + 64, S * (u % 8):S * (u % 8) + S],
                                  hc[:, S * u:S * u + S], const(name), start=True, stop=True)
                last.then_inc(ht_mm, 1)

            def mix2(n):
                w = min(512, UV - 512 * n)
                pe.wait_ge(gelu1, NB * n + NB)
                if n >= 2:
                    pe.wait_ge(m2_ev, n - 1)
                for b in range(NB):
                    last = mm(bank[n % 2][H0 * b:H0 * b + H0, 0:w], wmix2[:, :, :].rearrange("p r c -> p (r c)"),
                              gl[:, n % 2, b, 0:w], start=True, stop=True)
                last.then_inc(m2_mm, 1)

            pe.wait_ge(setup_dve, 3)
            pe.wait_ge(f2_ev, 4)
            for i in range(3 * NX):
                lo = CONST["tapsel"][0] + KW * i
                mm(bank[3][0:KW, H0 * i:H0 * i + H0], K[0:TAPS, lo:lo + KW], dw9[:, :], start=True, stop=True)
            mm(bank[3][0:KW, 384:384 + H0], const("rep", C), feg[:, :], start=True, stop=False)
            mm(bank[3][0:KW, 384:384 + H0], brep[:, :], fe[:, :], start=False, stop=False)
            mm(bank[3][0:KW, 384:384 + H0], one1[:, :], bfe[:, :], start=False, stop=True).then_inc(setup_pe, 1)
            for n in range(5):
                w = min(512, UV - 512 * n)
                pe.wait_ge(f2_ev, 5)
                for b in range(NB):
                    if n >= 1:
                        pe.wait_ge(gelu1, NB * (n - 1) + b + 1)
                    if n == 0:
                        mm(bank[4 + b][:, 0:1], fc2[:, :, :].rearrange("h s n -> h (s n)"), cols[0:H0, chb:chb + 1],
                           start=True, stop=True)
                    last = mm(bank[4 + b][:, 0:w], wmix1[:, b].rearrange("p s n -> p (s n)"), sp[:, 512 * n:512 * n + w],
                              start=(n > 0), stop=True, skip_group_check=(n == 0))
                    last.then_inc(m1_mm, 1)
                if n >= 1:
                    mix2(n - 1)
                if n == 2:
                    pe.wait_ge(setup_dve, 4)
                if n >= 2:
                    ht_step(n - 2)
            mix2(4)
            ht_step(3)
            ht_step(4)
            pe.wait_ge(ht_ev, 5)
            pe.wait_ge(ht_zero, 1)
            pe.wait_ge(m2_ev, 5)
            for j in range(8):
                g, c4 = divmod(j, 4)
                for c in range(4):
                    for b2 in range(2):
                        last = mm(bank[j][64 * b2:64 * b2 + 64, P * c:P * c + P], ht[:, :, C * (2 * g + b2) + 4 * c4 + c], const("ev"),
                                  start=True, stop=True)
                last.then_inc(i1_mm, 1)
            for j in range(4):
                pe.wait_ge(i1_dve, j + 1)
                pe.wait_ge(i1_act, j + 1)
                for r, name in enumerate(("e2re", "e2im")):
                    last = mm(bank[j][:, :], const(name), yy[:, 2 * j:2 * j + 2, :, r, :].rearrange("p j q x -> p (j q) x"),
                              start=(r == 0), stop=(r == 1))
                last.then_inc(i2_mm, 1)
            pe.wait_ge(x1_done, 4)
            for j in range(8):
                g, t4 = divmod(j, 4)
                pe.wait_ge(z_done, G2 + g + 1)
                for t in range(4):
                    x0 = NX * (4 * t4 + t)
                    last = pe.transpose(bank[j][0:WJ * C, P * t:P * t + P], zp[:, g, x0:x0 + WJ, :].rearrange("p x c -> p (x c)"), const("ident"))
                last.then_inc(w_mm, 1)
            pe.wait_ge(ld_q, 96)
            pe.wait_ge(w_dve, 5)
            pe.wait_ge(w_act, 4)
            for q in range(2):
                last = pe.transpose(bank[7][0:HID // 2, C * q:C * q + C], hid[:, 96 * q:96 * q + 96], K[0:C, CONST["ident"][0]:CONST["ident"][0] + C])
            last.then_inc(w_mm, 1)
            pe.wait_ge(hidt_done, 1)
            for s, (lo, hi) in enumerate(((0, 5), (5, 9))):
                if s:
                    pe.wait_ge(setup_pool, 10)
                for t in range(lo, hi):
                    for q in range(2):
                        last = mm(bank[4 + (t - lo) // 2][0:C, 192 * ((t - lo) % 2):192 * ((t - lo) % 2) + 192], hidT[:, q, :], wq[:, q, t, :],
                                  start=(q == 0), stop=(q == 1))
                last.then_inc(setup_pe, 1)
            pe.wait_ge(w_dve, 5)
            pe.wait_ge(ld_ones, 16)
            for j in range(8):
                if j >= 4:
                    pe.wait_ge(gelu2, j - 3)
                for dy in range(3):
                    last = mm(bank[j % 4][:, :], wdw[:, dy].rearrange("p x h -> p (x h)"), uw[0:KW, 2 * j:2 * j + 2, :, dy:dy + S],
                              start=(dy == 0), stop=(dy == 2))
                last.then_inc(dw_mm, 1)
            pe.wait_ge(setup_dve, 5)
            pe.wait_ge(ld_wfp, 16 * NX)
            for j in range(8):
                g, t4 = divmod(j, 4)
                pe.wait_ge(gelu2, min(8, 2 * t4 + 2) if g == 0 else 8)
                if j >= 4:
                    pe.wait_ge(x2_done, j - 3)
                for t in range(4):
                    last = mm(bank[4 + j % 4][:, FPN * t:FPN * (t + 1)], gd[:, 4 * t4 + t, 2 * g:2 * g + 2, :].rearrange("p b y -> p (b y)"),
                              wfp[:, :], start=True, stop=True)
                last.then_inc(fp_mm, 1)
            for j in range(4):
                g = j // 2
                pe.wait_ge(xn_done, g + 1)
                for t in range(4):
                    x0 = 8 * (4 * (j % 2) + t)
                    last = pe.transpose(bank[j][:, P * t:P * t + P], xc[:, g, x0:x0 + 8, :].rearrange("p x c -> p (x c)"), const("ident"))
                last.then_inc(tr_mm, 1)

            pe.wait_ge(tr_ev, 4)
            pe.wait_ge(ld_wc, 16 * 2 * TAPS)
            pe.wait_ge(x2_done, 8)
            for n in range(32 + 9):
                if n < 32:
                    u, k = divmod(n, 4)
                    b, yh = divmod(u, 2)
                    pe.wait_ge(tiled, n + 1)
                    if n >= 2:
                        pe.wait_ge(qk_ev, n - 1)
                    for t in range(4):
                        for hf in range(2):
                            last = mm(bank[n % 2][:, P * t:P * t + P], tile[:, n % 2, hf, t, :], wc[:, hf, 0:2 * CH],
                                      start=(hf == 0), stop=(hf == 1))
                    last.then_inc(qk_mm, 1)
                    if n >= 1:
                        pe.wait_ge(v_ev, n)
                    for hf in range(2):
                        for h in range(2):
                            src = tile[:, n % 2, hf, h::2, :]
                            last = mm(bank[2][64 * h:64 * h + 64, 0:256], wc[:, hf, 2 * CH:3 * CH], src, start=(hf == 0), stop=(hf == 1))
                    last.then_inc(v_mm, 1)
                m = n - 1
                if 0 <= m < 32:
                    pe.wait_ge(qk_ev, m + 1)
                    if m >= 1:
                        pe.wait_ge(prod, m)
                        pe.wait_ge(k_ev, m)
                    mm(bank[3][:, 0:256], const("dq"), qk[:, m % 2, :, 0:CH], start=True, stop=True)
                    mm(bank[4][:, 0:256], const("dq"), qk[:, m % 2, :, CH:2 * CH], start=True, stop=True)
                    mm(bank[4][:, 256:512], const("dks"), qk[:, m % 2, :, CH:2 * CH], start=True, stop=True).then_inc(f_mm, 1)
                m = n - 2
                if 0 <= m < 32:
                    pe.wait_ge(prod, m + 1)
                    if m >= 1:
                        pe.wait_ge(o_ev, m)
                    for p in range(2):
                        for s, name in enumerate(("im1", "im2")):
                            last = mm(bank[5][:, P * p:P * p + P], pr[:, m % 2, s, 2 * p:2 * p + 2, :].rearrange("p t c -> p (t c)"),
                                      const(name), start=(s == 0), stop=(s == 1))
                    last.then_inc(o_mm, 1)
                if n >= 8 and (n - 8) % 4 == 0 and (n - 8) // 4 < 8:
                    u = (n - 8) // 4
                    q = u % 4
                    pe.wait_ge(ft_done, u + 1)
                    for e in range(8):
                        src = stt[:, 7, 32 * e:32 * e + 32]
                        last = mm(bank[6 + e // 4][32 * q:32 * q + 32, P * (e % 4):P * (e % 4) + P], src, const("ident"), start=True, stop=True)
                    last.then_inc(t_mm, 1)
                if n >= 6 and (n - 6) % 4 == 0 and (n - 6) // 4 < 8:
                    u = (n - 6) // 4
                    if u >= 1:
                        pe.wait_ge(out_add, u)
                    pe.wait_ge(vo_done, 4 * u + 4)
                    pe.wait_ge(osq, 4 * u + 4)
                    for dst, lo, w, src in ((6, 0, const("mean"), os_), (6, 256, const("mean"), oq), (7, 0, wo1[:, :, :], vo), (7, 256, wo1[:, :, :], vs)):
                        for k in range(4):
                            last = mm(bank[dst][32 * k:32 * k + 32, lo:lo + 256], w, src[:, u % 2, k, :], start=True, stop=True)
                    last.then_inc(r_mm, 1)
                if n >= 7 and (n - 7) % 4 == 0 and (n - 7) // 4 < 8:
                    u = (n - 7) // 4
                    pe.wait_ge(r_var, u + 1)
                    for k in range(4):
                        last = mm(bank[6][32 * k:32 * k + 32, 0:256], wo2[:, :, :], vs[:, u % 2, k, :], start=True, stop=True)
                    last.then_inc(c_mm, 1)


_INS = ['x', 'L0_conv_g1', 'L0_conv_b1', 'L0_conv_g2', 'L0_conv_b2', 'L0_conv_w_te', 'L0_conv_b_te', 'L0_conv_w_fc',
        'L0_conv_b_fc', 'L0_conv_w_tp', 'L0_conv_b_tp', 'L0_conv_w_fe', 'L0_conv_b_fe', 'L0_conv_w_dw', 'L0_conv_b_dw',
        'L0_conv_w_fp', 'L0_conv_b_fp', 'L1_conv_w_hidden', 'L1_conv_w_qkv', 'L1_conv_w_out', 'L1_conv_ln1_scale',
        'L1_conv_ln1_bias', 'L1_conv_ln2_scale', 'L1_conv_ln2_bias']


def kernel(**inputs):
    import concourse.bacc as _bacc
    from concourse.bass_utils import run_bass_kernel_spmd as _run

    nc = _bacc.Bacc("TRN2", target_bir_lowering=False, num_devices=1)
    arrays, ins = {}, {}
    for name in _INS:
        a = np.ascontiguousarray(inputs[name])
        arrays["in_" + name] = a
        ins[name] = nc.dram_tensor("in_" + name, a.shape, F32, kind="ExternalInput").ap()
    k, ones = constants()
    extra = []
    for name, a in (("consts", k), ("ones_rows", ones)):
        arrays[name] = a
        extra.append(nc.dram_tensor(name, a.shape, F32, kind="ExternalInput").ap())
    out = nc.dram_tensor("out", (NB, S, S, C), F32, kind="ExternalOutput").ap()
    two_blocks(nc, ins, *extra, out)
    r = _run(nc, [arrays], core_ids=[0])
    return r.results[0]["out"]
```

```python
from contextlib import ExitStack

import numpy as np
import concourse.bass as bass
from concourse import mybir

F32 = mybir.dt.float32
ACT = mybir.ActivationFunctionType
ALU = mybir.AluOpType
AX = mybir.AxisListType

P = 128
NB, S, C = 4, 64, 16
G2 = NB // 2
H0 = 32
U = S // 2 + 1
S2 = S + 2
HID = 192
CH = HID // 3
SL, NC = 32, 30
TAPS = 9
KH = TAPS * C // 2
UV = U * S
EPS0, EPS1 = 1e-3, 1e-6
NX = 4
NW = S // NX
WJ = NX + 2
KW = WJ * C + WJ
WARM = 6
FPN = 96

def columns(*sizes):
    at, place = 0, {}
    for name, n in sizes:
        place[name] = (at, at + n)
        at += n
    return place, at


FIRST, NFIRST = columns(("f1c", 2 * U), ("f1s", 2 * U), ("mask", 2 * NB), ("sign", 1))
MORE, NMORE = columns(("dre", S), ("dim", S), ("selre", S), ("selim", S), ("ev", 2 * S), ("e2re", P), ("e2im", P), ("ident", P),
                      ("dq", P), ("inv", P), ("mean", 2 * C))
TAPC, NTAPC = columns(("tapsel", 3 * NX * KW), ("rep", KW), ("onessel", KW), ("one1", KW))
HALVES = [[(t, C * (t % 4), 0, C) for t in range(4 * hf, 4 * hf + 4)] + [(8, 4 * C, 8 * hf, 8)] for hf in range(2)]
HW = 2 * KH - C
VECS = "b_te b1 g1 b_fc g2 b2 b_dw ln2_scale ln2_bias ln1_scale ln1_bias".split()
WTS, NWTS = columns(("teT", NB * C), ("te", H0), ("fc", 4 * H0), ("fc2", 4 * H0), ("vecs", len(VECS)), ("tp", 2 * C), ("fe", H0),
                    ("bfe", H0), ("dw9", H0), ("wfp", FPN), ("wo", 2 * C), ("b_tp", C), ("b_fp", C), ("hid", 2 * (HW + 2 * KH)))


def constants():
    first, more, taps = np.zeros((P, NFIRST)), np.zeros((P, NMORE)), np.zeros((C, NTAPC))

    def put(name, a):
        for place, k in ((FIRST, first), (MORE, more), (TAPC, taps)):
            if name in place:
                lo, hi = place[name]
                k[:a.shape[0], lo:hi] = a.reshape(a.shape[0], hi - lo)

    n = np.arange(S)
    th = 2 * np.pi * np.outer(n, np.arange(U)) / S
    eye2 = np.eye(2)
    put("f1c", np.einsum("ab,yu->aybu", eye2, np.cos(th)).reshape(P, 2 * U))
    put("f1s", np.einsum("ab,yu->aybu", eye2, -np.sin(th)).reshape(P, 2 * U))
    ph = 2 * np.pi * np.outer(n, n) / S
    co, si = np.cos(ph), np.sin(ph)
    put("dre", np.concatenate([co, si]))
    put("dim", np.concatenate([-si, co]))
    mask = np.zeros((2, NB, C, 2, NB))
    for b in range(NB):
        mask[:, b, :, 0, b] = 1
        mask[0, b, :, 1, b] = 1
        mask[1, b, :, 1, b] = -1
    put("mask", mask.reshape(P, 2 * NB))
    sign = np.ones((P, 1))
    sign[3 * H0:] = -1
    put("sign", sign)
    sel = np.zeros((2, NB, 2, C, NB, C))
    for r in range(2):
        for b in range(NB):
            sel[r, b, r, :, b, :] = np.eye(C)
    put("selre", sel[0].reshape(P, S))
    put("selim", sel[1].reshape(P, S))
    put("ev", np.block([[co, si], [-si, co]]))
    w = np.zeros(S)
    w[:U] = 2
    w[0] = w[U - 1] = 1
    w = w * 0.5 / (S * S)
    put("e2re", np.kron(eye2, w[:, None] * co))
    put("e2im", np.kron(eye2, -w[:, None] * si))
    put("ident", np.eye(P))
    slots, real = [], [(0, 0), (0, 4), (4, 0), (4, 4)]
    for a in range(8):
        for b in range(8):
            if (a, b) not in real and ((-a) % 8, (-b) % 8) > (a, b):
                slots.append((a, b))
    pr, pc = np.meshgrid(np.arange(8), np.arange(8), indexing="ij")
    ang = lambda f: 2 * np.pi * (f[0] * pr + f[1] * pc).ravel() / 8
    fr, fi, ir, ii = (np.zeros((32, 64)) for _ in range(4))
    for s, f in enumerate(slots):
        fr[s], fi[s] = np.cos(ang(f)), -np.sin(ang(f))
        ir[s], ii[s] = 2 * np.cos(ang(f)) / 64, -2 * np.sin(ang(f)) / 64
    for s, (f, h) in enumerate(((real[0], real[1]), (real[2], real[3])), start=len(slots)):
        fr[s], fi[s] = np.cos(ang(f)), np.cos(ang(h))
        ir[s], ii[s] = np.cos(ang(f)) / 64, np.cos(ang(h)) / 64
    def tile(m):
        t = np.zeros((8, 2, 8, 2, 64))
        for q in range(2):
            t[:, q, :, q, :] = m.reshape(64, 8, 8).transpose(2, 1, 0)
        return t.reshape(P, P)
    put("dq", tile(np.concatenate([fr, fi])))
    put("inv", tile(np.concatenate([ir, ii])).T)
    put("mean", np.kron(eye2, np.full((CH, C), 1 / CH)))
    ts = np.zeros((3, 3, 3, NX, KW))
    for dy in range(3):
        for dx in range(3):
            for xx in range(NX):
                j = xx + dx
                ts[dy, dx, dy, xx, j * C:(j + 1) * C] = 1
                ts[dy, dx, dy, xx, WJ * C + j] = 1
    put("tapsel", ts.reshape(TAPS, -1))
    put("rep", np.concatenate([np.tile(np.eye(C), (1, WJ)), np.zeros((C, WJ))], 1))
    put("onessel", np.concatenate([np.zeros((C, WJ * C)), np.ones((C, WJ))], 1))
    put("one1", np.concatenate([np.zeros((1, WJ * C)), np.ones((1, WJ))], 1))
    ones = np.zeros((WJ, NW, NB, S2))
    for j in range(WJ):
        for t in range(NW):
            if 0 <= NX * t - 1 + j < S:
                ones[j, t, :, 1:S + 1] = 1
    return [a.astype(np.float32) for a in (first, more, taps, ones.reshape(WJ, -1))]


def laid_out(i):
    w = np.zeros((P, NWTS), np.float32)

    def put(name, a, row=0, at=0):
        lo = WTS[name][0] + at
        w[row:row + a.shape[0], lo:lo + a.shape[1]] = a

    for b in range(NB):
        put("teT", i["L0_conv_w_te"].T, at=C * b)
    put("te", i["L0_conv_w_te"])
    for r in range(2):
        put("fc", i["L0_conv_w_fc"][H0 * r:H0 * r + H0], at=2 * H0 * r)
        put("fc2", i["L0_conv_w_fc"][0:H0], at=2 * H0 * r)
    copies = {"g1": 8, "b_fc": 2, "b_dw": 4, "ln2_scale": 2, "ln2_bias": 2, "ln1_scale": 8, "ln1_bias": 8}
    for n, v in enumerate(VECS):
        a = i[("L1_conv_" if v.startswith("ln") else "L0_conv_") + v]
        put("vecs", np.tile(a, copies.get(v, 1))[:, None], at=n)
    for q in range(4):
        put("tp", i["L0_conv_w_tp"], H0 * q, C * (q % 2))
        put("wfp", i["L0_conv_w_fp"], H0 * q, C * q)
    for h in range(2):
        put("wo", i["L1_conv_w_out"], CH * h, C * h)
    put("fe", i["L0_conv_w_fe"])
    put("bfe", i["L0_conv_b_fe"][None])
    put("dw9", i["L0_conv_w_dw"].reshape(TAPS, H0))
    put("b_tp", np.broadcast_to(i["L0_conv_b_tp"], (P, C)))
    put("b_fp", np.broadcast_to(i["L0_conv_b_fp"], (P, C)))
    for q in range(2):
        hid = i["L1_conv_w_hidden"][:, 96 * q:96 * q + 96].T
        put("hid", hid, at=(HW + 2 * KH) * q + KH - C)
        for hf in range(2):
            put("hid", hid[:, 8 * hf:8 * hf + 8], at=(HW + 2 * KH) * q + HW + KH * hf + KH - 8)
    wq = i["L1_conv_w_qkv"].transpose(2, 1, 0, 3).reshape(2, HID // 2, TAPS * HID).transpose(1, 0, 2)
    return w, np.ascontiguousarray(wq)


def two_blocks(nc, x, weights, wqkv, first, more, taps, ones_rows, out):
    with ExitStack() as ctx:
        def sb(name, shape):
            return ctx.enter_context(nc.sbuf_tensor(name, shape, F32))

        def sem(name):
            return ctx.enter_context(nc.semaphore(name))

        bank = [ctx.enter_context(nc.psum_tensor(f"bank{i}", [P, 512], F32)) for i in range(8)]
        padded = nc.dram_tensor("padded", (C, NB, S2, S2), F32, kind="Internal").ap()

        kf, km, kt, wt = sb("kf", [P, NFIRST]), sb("km", [P, NMORE]), sb("kt", [C, NTAPC]), sb("wt", [P, NWTS])

        def const(name, rows=P):
            for place, k in ((FIRST, kf), (MORE, km), (TAPC, kt), (WTS, wt)):
                if name in place:
                    lo, hi = place[name]
                    return k[0:min(rows, k.shape[0]), lo:hi]

        def vec(name, rows=P):
            n = WTS["vecs"][0] + VECS.index(name)
            return wt[0:rows, n:n + 1]

        xt = sb("xt", [P, G2, S, C])
        x1 = sb("x1", [P, G2, S, C])
        x2 = sb("x2", [P, G2, S, C])
        xc = sb("xc", [P, G2, S, C])
        sq = sb("sq", [P, G2, S, C])
        zp = sb("zp", [P, G2, S2, C])
        st = sb("st", [P, G2, 4, S])
        spec = sb("spec", [P, 2 * UV])
        f1 = spec[:, 0:UV].rearrange("p (u b c) -> p u b c", u=U, b=NB)
        hc = spec[:, UV:2 * UV]
        tr = sb("tr", [P, G2, 8, 2, S])
        UW = S * S2
        arena = sb("arena", [P, 4 * UW])
        sp = arena[:, 0:UV]
        gl = arena[:, 2176:2176 + 4096].rearrange("p (i b n) -> p i b n", i=2, b=NB)
        ht = arena[:, 6272:6272 + 4096].rearrange("p (u n) -> p u n", u=S)
        yy = arena[:, 10368:10368 + 4096].rearrange("p (j q r x) -> p j q r x", j=8, q=4, r=2)
        uw = arena[:, 0:NW * NB * S2].rearrange("p (t b y) -> p t b y", t=NW, b=NB)
        gd = arena[:, 4224:4224 + NW * NB * S].rearrange("p (t b y) -> p t b y", t=NW, b=NB)
        ui = arena[0:KH, :].rearrange("p (i h x y) -> p i h x y", i=2, h=2, x=S)

        smix = sb("smix", [P, 2 * NB])
        wmix1 = sb("wmix1", [P, NB, 2, 2 * H0])
        hb = sb("hb", [H0, 2])
        wmix2 = sb("wmix2", [P, 2 * C])
        feg = sb("feg", [C, H0])
        brep = sb("brep", [C, KW])
        wfe = sb("wfe", [KW, H0])
        wdw = sb("wdw", [KW, 3, NX, H0])
        wq = sb("wq", [HID // 2, 2, TAPS, HID])
        wc = sb("wc", [KH, 2, HID])
        wo1 = sb("wo1", [P, 2 * C])
        wo2 = sb("wo2", [P, 2 * C])
        eps = sb("eps", [P, 2 + 8])
        tile = sb("tile", [KH, 2, 2, 4, P])
        qk = sb("qk", [P, 2, 2, 4, CH])
        kh = sb("kh", [P, 2, 4, 3, SL])
        tp = sb("tp", [P, 2, 2, 4, 2, SL])
        pr = sb("pr", [P, 2, 4, 2, SL])
        prt = sb("prt", [P, 2, 2 * P])
        four = lambda a: a.rearrange("p (i k n) -> p i k n", i=2, k=4)
        vs, os_ = four(spec[:, 0:2048]), four(spec[:, UV:UV + 2048])
        oq = four(sq[:, :, :, :].rearrange("p g x c -> p (g x c)"))
        vo = four(zp[:, :, :, :].rearrange("p g x c -> p (g x c)")[:, 0:2048])
        stt = x1[:, :, :, :].rearrange("p g x c -> p (g x c)").rearrange("p (s n) -> p s n", s=8)
        ot = xt

        ld_x0, ld_x1, ld_first, ld_more, ld_taps, ld_w, ld_q, ld_ones, ld_zero = map(
            sem, "ld_x0 ld_x1 ld_first ld_more ld_taps ld_w ld_q ld_ones ld_zero".split())
        ready0 = sem("ready0")
        smix_done, te_mm, dw_w_mm, wc_mm = map(sem, "smix_done te_mm dw_w_mm wc_mm".split())
        fe_ready, mix_ready, wfe_ready, wdw_ready, wc_ready, wo_ready = map(
            sem, "fe_ready mix_ready wfe_ready wdw_ready wc_ready wo_ready".split())
        chain, act_chain = sem("chain"), sem("act_chain")
        centred, squared, var_sum, sd_done, z_done = map(sem, "centred squared var_sum sd_done z_done".split())
        f1_mm, f1_dve, f1_act, f2_mm, f2_ev = map(sem, "f1_mm f1_dve f1_act f2_mm f2_ev".split())
        m1_mm, gelu1, m2_mm, m2_ev, ht_mm, ht_ev = map(sem, "m1_mm gelu1 m2_mm m2_ev ht_mm ht_ev".split())
        i1_mm, i1_dve, i1_act, i2_mm, x1_done = map(sem, "i1_mm i1_dve i1_act i2_mm x1_done".split())
        xb_done, zp_zero, x1b_done, uw_zero = map(sem, "xb_done zp_zero x1b_done uw_zero".split())
        w_mm, w_act, w_dve = sem("w_mm"), sem("w_act"), sem("w_dve")
        dw_mm, gelu2, fp_mm, x2_done = sem("dw_mm"), sem("gelu2"), sem("fp_mm"), sem("x2_done")
        tr_mm, tr_ev = sem("tr_mm"), sem("tr_ev")
        st_dma = [sem(f"st_dma{b}") for b in range(NB)]
        im_ld = [sem("im_ld0"), sem("im_ld1")]
        tiled, qk_mm, qk_ev, v_mm, v_ev = sem("tiled"), sem("qk_mm"), sem("qk_ev"), sem("v_mm"), sem("v_ev")
        f_mm, k_ev, prod, comb, p_mm, p_ev, o_mm, o_ev, osq, vo_done = map(
            sem, "f_mm k_ev prod comb p_mm p_ev o_mm o_ev osq vo_done".split())
        r_mm, r_act, r_var, r_sd, c_mm, ft_done, t_mm, out_add, out_st = map(
            sem, "r_mm r_act r_var r_sd c_mm ft_done t_mm out_add out_st".split())

        block = ctx.enter_context(nc.Block())

        def spans(n):
            return slice(512 * n, min(512 * n + 512, UV))

        def f1_evac(copy, j):
            g, c4 = divmod(j, 4)
            src = bank[j][:, 0:4 * 2 * U].rearrange("p (c b u) -> p c b u", c=4, b=2)
            return copy(f1[:, :, 2 * g:2 * g + 2, 4 * c4:4 * c4 + 4].rearrange("p u b c -> p c b u"), src)

        def w_evac(copy, j):
            g, t4 = divmod(j, 4)
            src = bank[t4][0:WJ * C, :].rearrange("p (t b y) -> p t b y", t=4, b=2)
            return copy(uw[0:WJ * C, 4 * t4:4 * t4 + 4, 2 * g:2 * g + 2, 1:S + 1], src)

        def gd_of(j):
            g, t4 = divmod(j, 4)
            return gd[:, 4 * t4:4 * t4 + 4, 2 * g:2 * g + 2, :]

        @block.sync
        def _(sp_):
            xin = x.rearrange("(g b) y x c -> g (b y) x c", g=G2)
            sp_.dma_start(xt[:, 0], xin[0]).then_inc(ld_x0, 16)
            sp_.dma_start(xt[:, 1], xin[1]).then_inc(ld_x1, 16)
            sp_.dma_start(km[:, :], more).then_inc(ld_more, 16)
            sp_.dma_start(wq[:, :, :, :].rearrange("p q t n -> p q (t n)"), wqkv).then_inc(ld_q, 16)
            sp_.wait_ge(m2_mm, 5)
            sp_.dma_start(uw[WJ * C:KW, :, :, :].rearrange("p t b y -> p (t b y)"), ones_rows).then_inc(ld_ones, 16)
            n = (S - 1) * S2 + S
            for b in range(NB):
                g, b2 = divmod(b, 2)
                sp_.wait_ge(ld_zero, 32)
                sp_.wait_ge(tr_ev, 2 * (g + 1))
                for xx in range(8):
                    dst = padded[:, b, 1 + xx:1 + xx + 57:8, 1:S + 1]
                    sp_.dma_start(dst, tr[C * xx:C * xx + C, g, :, b2, :]).then_inc(st_dma[b], 16)
                if b >= 2:
                    sp_.wait_ge(tiled, 8 * (b - 1))
                sp_.wait_ge(st_dma[b], 16 * 8)
                if b == 1:
                    sp_.wait_ge(fp_mm, 8)
                for hf in range(2):
                    for t, row, c0, n_c in HALVES[hf]:
                        dx, dy = divmod(t, 3)
                        src = padded[c0:c0 + n_c, b].rearrange("c x y -> c (x y)")[:, dx * S2 + dy:dx * S2 + dy + n]
                        sp_.dma_start(ui[row:row + n_c, 1 - b % 2, hf].rearrange("p x y -> p (x y)")[:, 0:n], src).then_inc(im_ld[b % 2], 16)
            ov = out.rearrange("(g b) y x c -> g (b y) x c", g=G2)
            for u in range(8):
                g, q = divmod(u, 4)
                sp_.wait_ge(out_add, u + 1)
                sp_.dma_start(ov[g, 32 * q:32 * q + 32], ot[32 * q:32 * q + 32, g]).then_inc(out_st, 16)
            sp_.wait_ge(out_st, 16 * 8)

        @block.gpsimd
        def _(pool):
            pool.memset(eps[:, 0:1], EPS0).then_inc(ready0, 1)
            pool.memset(eps[:, 1:2], EPS1).then_inc(ready0, 1)
            pool.memset(tr[:, :, :, :, :], 0.0).then_inc(ready0, 1)
            pool.memset(ht[:, U:S, :], 0.0).then_inc(ready0, 1)
            pool.memset(zp[:, :, 0:S2:S2 - 1, :], 0.0).then_inc(zp_zero, 1)
            pool.wait_ge(ld_first, 16)
            pool.wait_ge(ld_w, 16)
            pool.tensor_scalar(smix[:, :], const("mask"), vec("g1"), None, ALU.mult).then_inc(smix_done, 1)
            pool.wait_ge(ready0, 4)
            zrow = tr[:, :, :, :, :].rearrange("p g x b y -> p (g x b y)")
            flat = padded.rearrange("c b x y -> (c b x y)")
            for lo in (0, P * 2048):
                n = min(P * 2048, C * NB * S2 * S2 - lo)
                if lo:
                    pool.wait_ge(ld_zero, 16)
                pool.dma_start(flat[lo:lo + n].rearrange("(p n) -> p n", p=P), zrow[:, 0:n // P]).then_inc(ld_zero, 16)
            def per_channel(name):
                return const(name).rearrange("p (a c) -> p a c", a=1).broadcast_to([P, S, C])

            for g in range(G2):
                pool.wait_ge(centred, g + 1)
                pool.tensor_tensor(xt[:, g], xt[:, g], per_channel("b_tp"), ALU.add).then_inc(xb_done, 1)
            pool.wait_ge(m2_mm, 5)
            pool.memset(uw[0:WJ * C, :, :, 0:S2:S2 - 1], 0.0).then_inc(uw_zero, 1)
            for g in range(G2):
                pool.wait_ge(centred, G2 + g + 1)
                pool.tensor_tensor(x1[:, g], x1[:, g], per_channel("b_fp"), ALU.add).then_inc(x1b_done, 1)

            def times_v(m):
                u, k = divmod(m, 4)
                pool.wait_ge(o_ev, m + 1)
                if u >= 2:
                    pool.wait_ge(r_mm, u - 1)
                pool.tensor_tensor(vo[:, u % 2, k, :], vs[:, u % 2, k, :], os_[:, u % 2, k, :], ALU.mult).then_inc(vo_done, 1)

            for m in range(32):
                pool.wait_ge(prod, m + 1)
                if m >= 2:
                    pool.wait_ge(p_mm, m - 1)
                t, o = tp[:, m % 2], pr[:, m % 2]
                pool.tensor_tensor(o[:, :, 0, 0:NC], t[:, 0, :, 0, 0:NC], t[:, 0, :, 1, 0:NC], ALU.subtract)
                pool.tensor_tensor(o[:, :, 1, 0:NC], t[:, 1, :, 0, 0:NC], t[:, 1, :, 1, 0:NC], ALU.add)
                pool.tensor_copy(o[:, :, :, NC:SL], t[:, 0, :, :, NC:SL]).then_inc(comb, 1)
                if m >= 1:
                    times_v(m - 1)
            times_v(31)

        @block.scalar
        def _(act):
            act.dma_start(kf[:, :], first).then_inc(ld_first, 16)
            act.dma_start(wt[:, :], weights).then_inc(ld_w, 16)
            act.dma_start(kt[:, :], taps).then_inc(ld_taps, 16)

            tables = []

            def load_table(func):
                act.activation(eps[:, 2 + len(tables):3 + len(tables)], eps[:, 0:1], func)
                tables.append(func)

            def square(k, g):
                act.wait_ge(centred, 2 * k + g + 1)
                act.activation(sq[:, g], xc[:, g], ACT.Square).then_inc(squared, 1)

            def deviation(k, g):
                act.wait_ge(var_sum, 2 * k + g + 1)
                act.activation(st[:, g, 2, :], st[:, g, 1, :], ACT.Sqrt, bias=eps[:, k // 2:k // 2 + 1], scale=1.0 / C).then_inc(sd_done, 1)

            act.wait_ge(ready0, 2)
            load_table(ACT.Sqrt)
            square(0, 0)
            square(0, 1)
            act.wait_ge(ld_w, 16)
            act.wait_ge(ld_taps, 16)
            act.activation(feg[:, :], const("fe", C), ACT.Copy, scale=vec("g2", C)).then_inc(fe_ready, 1)
            act.activation(brep[:, :], const("onessel", C), ACT.Copy, scale=vec("b2", C)).then_inc(fe_ready, 1)
            deviation(0, 0)
            deviation(0, 1)
            act.activation(wo1[:, :], const("wo"), ACT.Copy, scale=vec("ln2_scale")).then_inc(wo_ready, 1)
            act.activation(wo2[:, :], const("wo"), ACT.Copy, scale=vec("ln2_bias")).then_inc(wo_ready, 1)
            act.wait_ge(ld_first, 16)
            act.activation(wmix2[:, :], const("tp"), ACT.Copy, scale=const("sign")).then_inc(mix_ready, 1)
            act.wait_ge(smix_done, 1)
            act.wait_ge(te_mm, 1)
            for b in range(NB):
                for s in range(2):
                    act.activation(wmix1[:, b, s, :], bank[7][:, 0:2 * H0], ACT.Copy,
                                   scale=smix[:, NB * s + b:NB * s + b + 1]).then_inc(mix_ready, 1)
            act.activation(hb[:, 0:1], bank[7][0:H0, 64:65], ACT.Identity, bias=vec("b_te", H0)).then_inc(act_chain, 1)
            act.wait_ge(act_chain, 1)
            act.activation(hb[:, 1:2], hb[:, 0:1], ACT.Copy, scale=float(S * S)).then_inc(mix_ready, 1)
            for j in range(1, 8, 2):
                act.wait_ge(f1_mm, j + 1)
                f1_evac(act.copy, j).then_inc(f1_act, 1)
            load_table(ACT.Gelu)
            for n in range(5):
                w = spans(n).stop - spans(n).start
                for b in range(NB):
                    act.wait_ge(m1_mm, NB * n + b + 1)
                    if n >= 2:
                        act.wait_ge(m2_mm, n - 1)
                    act.activation(gl[:, n % 2, b, 0:w], bank[4 + b][:, 0:w], ACT.Gelu, bias=vec("b_fc")).then_inc(gelu1, 1)
            load_table(ACT.Sqrt)
            for j in (1, 3, 4, 5, 6, 7):
                act.wait_ge(i1_mm, j + 1)
                act.copy(yy[:, j].rearrange("p q r x -> p (q r x)"), bank[j % 4][:, :]).then_inc(i1_act, 1)
            square(1, 0)
            deviation(1, 0)
            for j in range(4):
                act.wait_ge(w_mm, j + 1)
                if j == 0:
                    act.wait_ge(m2_mm, 5)
                w_evac(act.copy, j).then_inc(w_act, 1)
            square(1, 1)
            deviation(1, 1)
            for g in range(G2):
                load_table(ACT.Gelu)
                for j in range(4 * g, 4 * g + 4):
                    act.wait_ge(dw_mm, j + 1)
                    act.activation(gd_of(j), bank[4 + j % 4][:, :].rearrange("p (t b y) -> p t b y", t=4, b=2),
                                   ACT.Gelu, bias=vec("b_dw")).then_inc(gelu2, 1)
                load_table(ACT.Sqrt)
                if g == 1:
                    act.wait_ge(wc_mm, 1)
                    act.copy(wc[:, :, :].rearrange("p h n -> p (h n)"), bank[2][0:KH, 0:2 * HID]).then_inc(wc_ready, 1)
                square(2, g)
                deviation(2, g)

            for n in range(32 + 7):
                if n < 32:
                    u, k = divmod(n, 4)
                    act.wait_ge(qk_mm, n + 1)
                    if n >= 2:
                        act.wait_ge(f_mm, n - 1)
                    act.copy(qk[:, n % 2].rearrange("p r t c -> p t r c"),
                             bank[n % 2][:, :].rearrange("p (t r c) -> p t r c", t=4, r=2)).then_inc(qk_ev, 1)
                    act.wait_ge(v_mm, n + 1)
                    if u >= 2:
                        act.wait_ge(c_mm, u - 1)
                        act.wait_ge(vo_done, 4 * u - 4)
                    act.copy(vs[:, u % 2, k, :], bank[2][:, 0:256]).then_inc(v_ev, 1)
                m = n - 2
                if 0 <= m < 32:
                    act.wait_ge(p_mm, m + 1)
                    if m >= 2:
                        act.wait_ge(o_mm, m - 1)
                    act.copy(prt[:, m % 2, :], bank[4][:, 0:2 * P]).then_inc(p_ev, 1)
                m = n - 1
                if 0 <= m < 32:
                    act.wait_ge(f_mm, m + 1)
                    if m >= 2:
                        act.wait_ge(prod, m - 1)
                    kf_ = bank[3][:, 256:512].rearrange("p (a r s) -> p a r s", a=4, r=2)
                    act.copy(kh[:, m % 2, :, 0:2, :], kf_)
                    act.copy(kh[:, m % 2, :, 2, :], kf_[:, :, 0, :]).then_inc(k_ev, 1)
                m = n - 2
                if 0 <= m < 32:
                    u, k = divmod(m, 4)
                    act.wait_ge(o_mm, m + 1)
                    if u >= 2:
                        act.wait_ge(r_mm, u - 1)
                        act.wait_ge(vo_done, 4 * u - 4)
                    act.copy(os_[:, u % 2, k, :], bank[5][:, 0:256]).then_inc(o_ev, 1)
                    act.wait_ge(o_ev, m + 1)
                    act.activation(oq[:, u % 2, k, :], os_[:, u % 2, k, :], ACT.Square).then_inc(osq, 1)
                if n >= 6 and (n - 6) % 4 == 0 and (n - 6) // 4 < 8:
                    u = (n - 6) // 4
                    act.wait_ge(r_mm, u + 1)
                    act.copy(stt[:, 0, :], bank[6][:, 0:256])
                    act.activation(stt[:, 1, :], bank[6][:, 0:256], ACT.Square).then_inc(r_act, 1)
                    act.wait_ge(r_var, u + 1)
                    act.activation(stt[:, 3, :], stt[:, 2, :], ACT.Sqrt, bias=eps[:, 1:2]).then_inc(r_sd, 1)

        @block.vector
        def _(dve):
            done = [0]

            def link(ins_):
                ins_.then_inc(chain, 1)
                done[0] += 1
                dve.wait_ge(chain, done[0])

            def bc(a):
                return a.rearrange("p (x a) -> p x a", a=1).broadcast_to([P, S, C])

            def centre(g, src):
                link(dve.tensor_reduce(out=st[:, g, 0, :], in_=src[:, g], axis=AX.X, op=ALU.add))
                dve.scalar_tensor_tensor(out=xc[:, g], in0=bc(st[:, g, 0, :]), scalar=-1.0 / C, in1=src[:, g],
                                         op0=ALU.mult, op1=ALU.add).then_inc(centred, 1)

            def normalise(k, g, dst):
                dve.wait_ge(squared, 2 * k + g + 1)
                dve.tensor_reduce(out=st[:, g, 1, :], in_=sq[:, g], axis=AX.X, op=ALU.add).then_inc(var_sum, 1)
                dve.wait_ge(sd_done, 2 * k + g + 1)
                link(dve.reciprocal(st[:, g, 3, :], st[:, g, 2, :]))
                dve.tensor_tensor(dst, xc[:, g], bc(st[:, g, 3, :]), ALU.mult).then_inc(z_done, 1)

            for g in range(G2):
                dve.wait_ge((ld_x0, ld_x1)[g], 16)
                centre(g, xt)
            for g in range(G2):
                normalise(0, g, sq[:, g])
            for j in range(0, 8, 2):
                dve.wait_ge(f1_mm, j + 1)
                f1_evac(dve.tensor_copy, j).then_inc(f1_dve, 1)
            for n in range(5):
                dve.wait_ge(f2_mm, n + 1)
                dve.tensor_copy(sp[:, spans(n)], bank[n][:, 0:spans(n).stop - spans(n).start]).then_inc(f2_ev, 1)
            for n in range(6):
                if n < 5:
                    dve.wait_ge(m2_mm, n + 1)
                    dve.tensor_copy(hc[:, spans(n)], bank[n % 2][:, 0:spans(n).stop - spans(n).start]).then_inc(m2_ev, 1)
                if n >= 1:
                    m = n - 1
                    w = spans(m).stop - spans(m).start
                    dve.wait_ge(ht_mm, m + 1)
                    dve.tensor_copy(ht[:, 8 * m:8 * m + w // S, :].rearrange("p u n -> p (u n)"),
                                    bank[2 + m % 2][:, 0:w]).then_inc(ht_ev, 1)
            for j in (0, 2):
                dve.wait_ge(i1_mm, j + 1)
                dve.tensor_copy(yy[:, j].rearrange("p q r x -> p (q r x)"), bank[j][:, :]).then_inc(i1_dve, 1)
            dve.wait_ge(dw_w_mm, 1)
            link(dve.tensor_copy(wfe[:, :], bank[6][0:KW, 384:384 + H0]))
            dve.tensor_tensor(wdw[:, :, :, :].rearrange("p a b h -> p (a b) h"), bank[6][0:KW, 0:384].rearrange("p (a h) -> p a h", h=H0),
                              wfe[:, :].rearrange("p (a h) -> p a h", a=1).broadcast_to([KW, 3 * NX, H0]), ALU.mult).then_inc(wdw_ready, 1)
            for g in range(G2):
                dve.wait_ge(xb_done, g + 1)
                for xh in range(2):
                    j = 2 * g + xh
                    cols = slice(32 * xh, 32 * xh + 32)
                    dve.wait_ge(i2_mm, j + 1)
                    o = dve.tensor_tensor(x1[:, g, cols, :], bank[4 + j][:, :].rearrange("p (c x) -> p x c", c=C),
                                          xt[:, g, cols, :], ALU.add)
                    o.then_inc(x1_done, 1)
                dve.wait_ge(x1_done, 2 * g + 2)
                centre(g, x1)
                if g == 0:
                    dve.wait_ge(zp_zero, 1)
                normalise(1, g, zp[:, g, 1:S + 1])
            for j in range(4, 8):
                dve.wait_ge(w_mm, j + 1)
                w_evac(dve.tensor_copy, j).then_inc(w_dve, 1)
            for g in range(G2):
                dve.wait_ge(x1b_done, g + 1)
                for j in range(4 * g, 4 * g + 4):
                    t4 = j % 4
                    tx = lambda a: a[:, g, 16 * t4:16 * t4 + 16, :].rearrange("p (t x) c -> p t (x c)", t=4)
                    dve.wait_ge(fp_mm, j + 1)
                    dve.tensor_tensor(tx(x2), bank[j][:, 0:4 * FPN].rearrange("p (t n) -> p t n", t=4)[:, :, 0:NX * C],
                                      tx(x1), ALU.add).then_inc(x2_done, 1)
                dve.wait_ge(x2_done, 4 * g + 4)
                centre(g, x2)
                normalise(2, g, xc[:, g])
                if g == 0:
                    dve.wait_ge(ld_zero, 32)
                for i in range(2):
                    dve.wait_ge(tr_mm, 2 * g + i + 1)
                    dve.tensor_scalar(tr[:, g, 4 * i:4 * i + 4], bank[2 * g + i][:, :].rearrange("p (t b y) -> p t b y", t=4, b=2),
                                      vec("ln1_scale"), vec("ln1_bias"), ALU.mult, ALU.add).then_inc(tr_ev, 1)

            def gather(n):
                u, k = divmod(n, 4)
                b, yh = divmod(u, 2)
                if n % 8 == 0:
                    dve.wait_ge(im_ld[b % 2], 16 * 10 * (b // 2 + 1))
                if n >= 2:
                    dve.wait_ge(v_mm, n - 1)
                for hf in range(2):
                    src = ui[:, 1 - b % 2, hf, 16 * k:16 * k + 16, 32 * yh:32 * yh + 32].rearrange("p x (t y) -> p t x y", t=2)
                    o = dve.tensor_copy(tile[:, n % 2, hf].rearrange("p (t h) (x y) -> p t (h x) y", t=2, x=8), src)
                o.then_inc(tiled, 1)

            gather(0)
            for n in range(32 + 9):
                if n + 1 < 32:
                    gather(n + 1)
                if n >= 7 and (n - 7) % 4 == 0 and (n - 7) // 4 < 8:
                    u = (n - 7) // 4
                    dve.wait_ge(r_sd, u + 1)
                    link(dve.reciprocal(stt[:, 5, :], stt[:, 3, :]))
                    link(dve.tensor_tensor(stt[:, 6, :], stt[:, 4, :], stt[:, 5, :], ALU.mult))
                m = n - 1
                if 0 <= m < 32:
                    dve.wait_ge(k_ev, m + 1)
                    if m >= 2:
                        dve.wait_ge(comb, m - 1)
                    for e in range(2):
                        o = dve.tensor_tensor(tp[:, m % 2, e].rearrange("p a r s -> p a (r s)"),
                                              bank[3][:, 0:256].rearrange("p (a n) -> p a n", a=4),
                                              kh[:, m % 2, :, e:e + 2, :].rearrange("p a r s -> p a (r s)"), ALU.mult)
                    o.then_inc(prod, 1)
                if n >= 7 and (n - 7) % 4 == 0 and (n - 7) // 4 < 8:
                    u = (n - 7) // 4
                    dve.wait_ge(c_mm, u + 1)
                    txy = lambda a: a.rearrange("p (t x y) -> p t x y", t=2, x=8)
                    dve.tensor_tensor(stt[:, 7, :].rearrange("p (x t y) -> p t x y", t=2, x=8), txy(bank[6][:, 0:256]),
                                      txy(stt[:, 6, :]), ALU.add).then_inc(ft_done, 1)
                if n >= 6 and (n - 6) % 4 == 0 and (n - 6) // 4 < 8:
                    u = (n - 6) // 4
                    dve.wait_ge(r_act, u + 1)
                    link(dve.tensor_tensor(stt[:, 2, :], bank[6][:, 256:512], stt[:, 1, :], ALU.subtract))
                    dve.tensor_scalar(stt[:, 2, :], stt[:, 2, :], 0.0, None, ALU.max).then_inc(r_var, 1)
                    link(dve.tensor_tensor(stt[:, 4, :], bank[7][:, 256:512], stt[:, 0, :], ALU.mult))
                    link(dve.tensor_tensor(stt[:, 4, :], bank[7][:, 0:256], stt[:, 4, :], ALU.subtract))
                if n >= 8 and (n - 8) % 4 == 0 and (n - 8) // 4 < 8:
                    u = (n - 8) // 4
                    g, q = divmod(u, 4)
                    dve.wait_ge(t_mm, u + 1)
                    rows = slice(32 * q, 32 * q + 32)
                    for i in range(2):
                        res = lambda a: a[rows, g].rearrange("p (k e) c -> p k e c", k=8)[:, :, 4 * i:4 * i + 4, :]
                        o = dve.tensor_tensor(res(ot), bank[6 + i][0:32, :].rearrange("p (e k c) -> p k e c", e=4, k=8),
                                              res(x2), ALU.add)
                    o.then_inc(out_add, 1)

        @block.tensor
        def _(pe):
            mm = pe.matmul
            def keep_warm(times):
                for _ in range(times):
                    mm(bank[6][:, :], ht[:, U:U + 2, :].rearrange("p u n -> p (u n)"), ht[:, U + 2:U + 10, :].rearrange("p u n -> p (u n)"),
                       start=True, stop=True)

            pe.wait_ge(ready0, 4)
            keep_warm(WARM)
            pe.wait_ge(ld_w, 16)
            fc = const("fc", H0).rearrange("h (r n) -> h r n", r=2)
            for r in range(2):
                mm(bank[7][64 * r:64 * r + 64, 0:2 * H0], const("teT", H0), fc[:, r, :], start=True, stop=True)
            mm(bank[7][0:H0, 64:65], const("te", C), vec("b1", C), start=True, stop=True).then_inc(te_mm, 1)
            def depthwise_weights():
                pe.wait_ge(ld_taps, 16)
                for i in range(3 * NX):
                    lo = TAPC["tapsel"][0] + KW * i
                    mm(bank[6][0:KW, H0 * i:H0 * i + H0], kt[0:TAPS, lo:lo + KW], const("dw9", TAPS), start=True, stop=True)
                pe.wait_ge(fe_ready, 2)
                mm(bank[6][0:KW, 384:384 + H0], const("rep", C), feg[:, :], start=True, stop=False)
                mm(bank[6][0:KW, 384:384 + H0], brep[:, :], const("fe", C), start=False, stop=False)
                mm(bank[6][0:KW, 384:384 + H0], const("one1", 1), const("bfe", 1), start=False, stop=True).then_inc(dw_w_mm, 1)

            def conv_weights():
                pe.wait_ge(ld_q, 16)
                pe.wait_ge(x2_done, 4)
                for hf in range(2):
                    for i, (t, row, _, n_c) in enumerate(HALVES[hf]):
                        for q in range(2):
                            lo = WTS["hid"][0] + (HW + 2 * KH) * q + (KH - C - row if n_c == C else HW + KH * hf)
                            last = mm(bank[2][0:KH, HID * hf:HID * hf + HID], wt[0:HID // 2, lo:lo + KH], wq[:, q, t, :],
                                      start=(i + q == 0), stop=(i == 4 and q == 1))
                last.then_inc(wc_mm, 1)

            pe.wait_ge(ld_first, 16)
            for j in range(8):
                g, c4 = divmod(j, 4)
                if j == 4:
                    keep_warm(1)
                if j == 7:
                    pe.wait_ge(mix_ready, 10)
                pe.wait_ge(z_done, g + 1)
                for c in range(4):
                    for r, name in enumerate(("f1c", "f1s")):
                        last = mm(bank[j][64 * r:64 * r + 64, 2 * U * c:2 * U * (c + 1)], sq[:, g, :, 4 * c4 + c], const(name),
                                  start=True, stop=True)
                last.then_inc(f1_mm, 1)
            pe.wait_ge(ld_more, 16)
            pe.wait_ge(f1_act, 4)
            pe.wait_ge(f1_dve, 4)
            for n in range(5):
                for u in range(8 * n, min(8 * n + 8, U)):
                    for r, name in enumerate(("dre", "dim")):
                        last = mm(bank[n][64 * r:64 * r + 64, S * (u % 8):S * (u % 8) + S],
                                  f1[:, u].rearrange("p b c -> p (b c)"), const(name), start=True, stop=True)
                last.then_inc(f2_mm, 1)

            def ht_step(m):
                pe.wait_ge(m2_ev, m + 1)
                if m >= 2:
                    pe.wait_ge(ht_ev, m - 1)
                for u in range(8 * m, min(8 * m + 8, U)):
                    for r, name in enumerate(("selre", "selim")):
                        last = mm(bank[2 + m % 2][64 * r:64 * r + 64, S * (u % 8):S * (u % 8) + S],
                                  hc[:, S * u:S * u + S], const(name), start=True, stop=True)
                last.then_inc(ht_mm, 1)

            def mix2(n):
                w = spans(n).stop - spans(n).start
                pe.wait_ge(gelu1, NB * n + NB)
                if n >= 2:
                    pe.wait_ge(m2_ev, n - 1)
                for b in range(NB):
                    last = mm(bank[n % 2][H0 * b:H0 * b + H0, 0:w], wmix2[:, :], gl[:, n % 2, b, 0:w], start=True, stop=True)
                last.then_inc(m2_mm, 1)

            for n in range(5):
                w = spans(n).stop - spans(n).start
                pe.wait_ge(f2_ev, 5 if n == 0 else n + 1)
                for b in range(NB):
                    if n >= 1:
                        pe.wait_ge(gelu1, NB * (n - 1) + b + 1)
                    if n == 0:
                        mm(bank[4 + b][:, 0:1], const("fc2", H0), hb[:, 1:2], start=True, stop=True)
                    mm(bank[4 + b][:, 0:w], wmix1[:, b].rearrange("p s n -> p (s n)"), sp[:, spans(n)],
                       start=(n > 0), stop=True, skip_group_check=(n == 0)).then_inc(m1_mm, 1)
                if n >= 1:
                    mix2(n - 1)
                if n >= 2:
                    ht_step(n - 2)
            mix2(4)
            ht_step(3)
            ht_step(4)
            depthwise_weights()
            pe.wait_ge(ht_ev, 5)
            pe.wait_ge(ready0, 4)
            for g in range(G2):
                for j in range(4 * g, 4 * g + 4):
                    for c in range(4):
                        for b2 in range(2):
                            last = mm(bank[j % 4][64 * b2:64 * b2 + 64, P * c:P * c + P], ht[:, :, C * (2 * g + b2) + 4 * (j % 4) + c],
                                      const("ev"), start=True, stop=True)
                    last.then_inc(i1_mm, 1)
                pe.wait_ge(i1_dve, 2)
                pe.wait_ge(i1_act, 2 + 4 * g)
                for j in range(2 * g, 2 * g + 2):
                    cols = slice(32 * (j % 2), 32 * (j % 2) + 32)
                    if j == 2:
                        pe.wait_ge(wdw_ready, 1)
                    for r, name in enumerate(("e2re", "e2im")):
                        src = yy[:, 4 * g:4 * g + 4, :, r, cols].rearrange("p j q x -> p (j q) x")
                        last = mm(bank[4 + j][:, :], const(name), src, start=(r == 0), stop=(r == 1))
                    last.then_inc(i2_mm, 1)

            def windows(g):
                pe.wait_ge(z_done, G2 + g + 1)
                for t4 in range(4):
                    if g == 1:
                        pe.wait_ge(w_act, t4 + 1)
                    for t in range(4):
                        x0 = NX * (4 * t4 + t)
                        last = pe.transpose(bank[t4][0:WJ * C, P * t:P * t + P], zp[:, g, x0:x0 + WJ, :].rearrange("p x c -> p (x c)"),
                                            const("ident"))
                    last.then_inc(w_mm, 1)

            def depthwise(j):
                g, t4 = divmod(j, 4)
                if g == 0:
                    pe.wait_ge(w_act, t4 + 1)
                    pe.wait_ge(x1_done, 4)
                else:
                    pe.wait_ge(w_dve, t4 + 1)
                    pe.wait_ge(gelu2, j - 3)
                for dy in range(3):
                    last = mm(bank[4 + t4][:, :], wdw[:, dy].rearrange("p x h -> p (x h)"), uw[0:KW, 4 * t4:4 * t4 + 4, 2 * g:2 * g + 2, dy:dy + S],
                              start=(dy == 0), stop=(dy == 2))
                last.then_inc(dw_mm, 1)

            def project(j):
                g, t4 = divmod(j, 4)
                pe.wait_ge(gelu2, j + 1)
                if g == 0:
                    pe.wait_ge(w_dve, t4 + 1)
                for t in range(4):
                    last = mm(bank[j][:, FPN * t:FPN * (t + 1)], gd[:, 4 * t4 + t, 2 * g:2 * g + 2, :].rearrange("p b y -> p (b y)"),
                              const("wfp"), start=True, stop=True)
                last.then_inc(fp_mm, 1)

            def channel_major(g):
                pe.wait_ge(z_done, 2 * G2 + g + 1)
                if g == 1:
                    pe.wait_ge(wc_ready, 1)
                for i in range(2):
                    for t in range(4):
                        x0 = 8 * (4 * i + t)
                        last = pe.transpose(bank[2 * g + i][:, P * t:P * t + P], xc[:, g, x0:x0 + 8, :].rearrange("p x c -> p (x c)"), const("ident"))
                    last.then_inc(tr_mm, 1)

            pe.wait_ge(i1_act, 6)
            windows(0)
            pe.wait_ge(uw_zero, 1)
            pe.wait_ge(ld_ones, 16)
            for j in range(4):
                depthwise(j)
            windows(1)
            depthwise(4)
            for j in range(4):
                project(j)
            for j in range(5, 8):
                depthwise(j)
            channel_major(0)
            for j in range(4, 8):
                project(j)
            conv_weights()
            channel_major(1)

            pe.wait_ge(tr_ev, 4)
            pe.wait_ge(x2_done, 8)
            pe.wait_ge(wo_ready, 2)
            for n in range(32 + 9):
                if n < 32:
                    u, k = divmod(n, 4)
                    b, yh = divmod(u, 2)
                    pe.wait_ge(tiled, n + 1)
                    if n >= 2:
                        pe.wait_ge(qk_ev, n - 1)
                    for t in range(4):
                        for hf in range(2):
                            last = mm(bank[n % 2][:, P * t:P * t + P], tile[:, n % 2, hf, t, :], wc[:, hf, 0:2 * CH],
                                      start=(hf == 0), stop=(hf == 1))
                    last.then_inc(qk_mm, 1)
                    if n >= 1:
                        pe.wait_ge(v_ev, n)
                    for hf in range(2):
                        for h in range(2):
                            src = tile[:, n % 2, hf, h::2, :]
                            last = mm(bank[2][64 * h:64 * h + 64, 0:256], wc[:, hf, 2 * CH:3 * CH], src, start=(hf == 0), stop=(hf == 1))
                    last.then_inc(v_mm, 1)
                m = n - 2
                if 0 <= m < 32:
                    pe.wait_ge(comb, m + 1)
                    if m >= 1:
                        pe.wait_ge(p_ev, m)
                    for t in range(2):
                        src = pr[:, m % 2, 2 * t:2 * t + 2].rearrange("p a r s -> p (a r s)")
                        last = pe.transpose(bank[4][:, P * t:P * t + P], src, const("ident"))
                    last.then_inc(p_mm, 1)
                m = n - 1
                if 0 <= m < 32:
                    pe.wait_ge(qk_ev, m + 1)
                    if m >= 1:
                        pe.wait_ge(prod, m)
                    for r in range(2):
                        for t in range(2):
                            src = qk[:, m % 2, r, 2 * t:2 * t + 2, :].rearrange("p t c -> p (t c)")
                            last = mm(bank[3][:, 256 * r + P * t:256 * r + P * t + P], src, const("dq"), start=True, stop=True)
                    last.then_inc(f_mm, 1)
                m = n - 2
                if 0 <= m < 32:
                    pe.wait_ge(p_ev, m + 1)
                    if m >= 1:
                        pe.wait_ge(o_ev, m)
                    for t in range(2):
                        last = mm(bank[5][:, P * t:P * t + P], prt[:, m % 2, P * t:P * t + P], const("inv"), start=True, stop=True)
                    last.then_inc(o_mm, 1)
                if n >= 8 and (n - 8) % 4 == 0 and (n - 8) // 4 < 8:
                    u = (n - 8) // 4
                    pe.wait_ge(ft_done, u + 1)
                    for e in range(8):
                        src = stt[:, 7, 32 * e:32 * e + 32]
                        last = pe.transpose(bank[6 + e // 4][0:32, P * (e % 4):P * (e % 4) + P], src, const("ident"))
                    last.then_inc(t_mm, 1)
                if n >= 6 and (n - 6) % 4 == 0 and (n - 6) // 4 < 8:
                    u = (n - 6) // 4
                    if u >= 1:
                        pe.wait_ge(out_add, u)
                    pe.wait_ge(vo_done, 4 * u + 4)
                    pe.wait_ge(osq, 4 * u + 4)
                    for dst, lo, w, src in ((6, 0, const("mean"), os_), (6, 256, const("mean"), oq), (7, 0, wo1[:, :], vo), (7, 256, wo1[:, :], vs)):
                        for k in range(4):
                            last = mm(bank[dst][32 * k:32 * k + 32, lo:lo + 256], w, src[:, u % 2, k, :], start=True, stop=True)
                    last.then_inc(r_mm, 1)
                if n >= 7 and (n - 7) % 4 == 0 and (n - 7) // 4 < 8:
                    u = (n - 7) // 4
                    pe.wait_ge(r_var, u + 1)
                    for k in range(4):
                        last = mm(bank[6][32 * k:32 * k + 32, 0:256], wo2[:, :], vs[:, u % 2, k, :], start=True, stop=True)
                    last.then_inc(c_mm, 1)


_INS = ['x', 'L0_conv_g1', 'L0_conv_b1', 'L0_conv_g2', 'L0_conv_b2', 'L0_conv_w_te', 'L0_conv_b_te', 'L0_conv_w_fc',
        'L0_conv_b_fc', 'L0_conv_w_tp', 'L0_conv_b_tp', 'L0_conv_w_fe', 'L0_conv_b_fe', 'L0_conv_w_dw', 'L0_conv_b_dw',
        'L0_conv_w_fp', 'L0_conv_b_fp', 'L1_conv_w_hidden', 'L1_conv_w_qkv', 'L1_conv_w_out', 'L1_conv_ln1_scale',
        'L1_conv_ln1_bias', 'L1_conv_ln2_scale', 'L1_conv_ln2_bias']


def kernel(**inputs):
    import concourse.bacc as _bacc
    from concourse.bass_utils import run_bass_kernel_spmd as _run

    nc = _bacc.Bacc("TRN2", target_bir_lowering=False, num_devices=1)
    given = {name: np.asarray(inputs[name]) for name in _INS}
    w, wq = laid_out(given)
    first, more, taps, ones = constants()
    arrays = {"x": np.ascontiguousarray(given["x"]), "weights": w, "w_qkv": wq, "first": first, "more": more, "taps": taps, "ones_rows": ones}
    args = [nc.dram_tensor(name, a.shape, F32, kind="ExternalInput").ap() for name, a in arrays.items()]
    out = nc.dram_tensor("out", (NB, S, S, C), F32, kind="ExternalOutput").ap()
    two_blocks(nc, *args, out)
    r = _run(nc, [arrays], core_ids=[0])
    return r.results[0]["out"]
```

```python
from contextlib import ExitStack

import numpy as np
import concourse.bass as bass
from concourse import mybir

F32, BF16 = mybir.dt.float32, mybir.dt.bfloat16
ACT = mybir.ActivationFunctionType
ALU = mybir.AluOpType
AX = mybir.AxisListType

P = 128
NB, S, C = 4, 64, 16
G2 = NB // 2
H0 = 32
U = S // 2 + 1
S2 = S + 2
HID = 192
CH = HID // 3
SL, NC = 32, 30
TAPS = 9
SLOTS = 8 + 2
PAD_STORES, PART_STORES, PART_LOADS = 3, 6, 3
FULL = P // C
UV = U * S
EPS0, EPS1 = 1e-3, 1e-6
NX = 4
NW = S // NX
WJ = NX + 2
KW = WJ * C + WJ
WARM = 7
FPN = 96

def columns(*sizes):
    at, place = 0, {}
    for name, n in sizes:
        place[name] = (at, at + n)
        at += n
    return place, at


FIRST, NFIRST = columns(("f1c", 2 * U), ("f1s", 2 * U), ("mask", 2 * NB), ("sign", 1))
MORE, NMORE = columns(("dre", S), ("dim", S), ("selre", S), ("selim", S), ("ev", 2 * S), ("e2re", P), ("e2im", P), ("ident", P),
                      ("dq", P), ("inv", P), ("mean", 2 * C))
TAPC, NTAPC = columns(("rep", KW), ("onessel", KW), ("one1", KW))
SPLIT = [(d, w) for w in range(3) for d in range(3) if (d, w) != (2, 2)]
VECS = "b_te b1 g1 b_fc g2 b2 b_dw ln2_scale ln2_bias ln1_scale ln1_bias".split()
WTS, NWTS = columns(("teT", NB * C), ("te", H0), ("fc", 4 * H0), ("fc2", 4 * H0), ("vecs", len(VECS)), ("tp", 2 * C), ("fe", H0),
                    ("bfe", H0), ("dw", 3 * NX * H0), ("wfp", FPN), ("wo", 2 * C), ("b_tp", C), ("b_fp", C), ("hid", 2 * H0))


def constants():
    first, more, taps = np.zeros((P, NFIRST)), np.zeros((P, NMORE)), np.zeros((C, NTAPC))

    def put(name, a):
        for place, k in ((FIRST, first), (MORE, more), (TAPC, taps)):
            if name in place:
                lo, hi = place[name]
                k[:a.shape[0], lo:hi] = a.reshape(a.shape[0], hi - lo)

    n = np.arange(S)
    th = 2 * np.pi * np.outer(n, np.arange(U)) / S
    eye2 = np.eye(2)
    put("f1c", np.einsum("ab,yu->aybu", eye2, np.cos(th)).reshape(P, 2 * U))
    put("f1s", np.einsum("ab,yu->aybu", eye2, -np.sin(th)).reshape(P, 2 * U))
    ph = 2 * np.pi * np.outer(n, n) / S
    co, si = np.cos(ph), np.sin(ph)
    put("dre", np.concatenate([co, si]))
    put("dim", np.concatenate([-si, co]))
    mask = np.zeros((2, NB, C, 2, NB))
    for b in range(NB):
        mask[:, b, :, 0, b] = 1
        mask[0, b, :, 1, b] = 1
        mask[1, b, :, 1, b] = -1
    put("mask", mask.reshape(P, 2 * NB))
    sign = np.ones((P, 1))
    sign[3 * H0:] = -1
    put("sign", sign)
    sel = np.zeros((2, NB, 2, C, NB, C))
    for r in range(2):
        for b in range(NB):
            sel[r, b, r, :, b, :] = np.eye(C)
    put("selre", sel[0].reshape(P, S))
    put("selim", sel[1].reshape(P, S))
    put("ev", np.block([[co, si], [-si, co]]))
    w = np.zeros(S)
    w[:U] = 2
    w[0] = w[U - 1] = 1
    w = w * 0.5 / (S * S)
    put("e2re", np.kron(eye2, w[:, None] * co))
    put("e2im", np.kron(eye2, -w[:, None] * si))
    put("ident", np.eye(P))
    slots, real = [], [(0, 0), (0, 4), (4, 0), (4, 4)]
    for a in range(8):
        for b in range(8):
            if (a, b) not in real and ((-a) % 8, (-b) % 8) > (a, b):
                slots.append((a, b))
    pr, pc = np.meshgrid(np.arange(8), np.arange(8), indexing="ij")
    ang = lambda f: 2 * np.pi * (f[0] * pr + f[1] * pc).ravel() / 8
    fr, fi, ir, ii = (np.zeros((32, 64)) for _ in range(4))
    for s, f in enumerate(slots):
        fr[s], fi[s] = np.cos(ang(f)), -np.sin(ang(f))
        ir[s], ii[s] = 2 * np.cos(ang(f)) / 64, -2 * np.sin(ang(f)) / 64
    for s, (f, h) in enumerate(((real[0], real[1]), (real[2], real[3])), start=len(slots)):
        fr[s], fi[s] = np.cos(ang(f)), np.cos(ang(h))
        ir[s], ii[s] = np.cos(ang(f)) / 64, np.cos(ang(h)) / 64
    def tile(m):
        t = np.zeros((8, 2, 8, 2, 64))
        for q in range(2):
            t[:, q, :, q, :] = m.reshape(64, 8, 8).transpose(2, 1, 0)
        return t.reshape(P, P)
    put("dq", tile(np.concatenate([fr, fi])))
    put("inv", tile(np.concatenate([ir, ii])).T)
    put("mean", np.kron(eye2, np.full((CH, C), 1 / CH)))
    put("rep", np.concatenate([np.tile(np.eye(C), (1, WJ)), np.zeros((C, WJ))], 1))
    put("onessel", np.concatenate([np.zeros((C, WJ * C)), np.ones((C, WJ))], 1))
    put("one1", np.concatenate([np.zeros((1, WJ * C)), np.ones((1, WJ))], 1))
    ones = np.zeros((WJ, NW, NB, S2))
    for j in range(WJ):
        for t in range(NW):
            if 0 <= NX * t - 1 + j < S:
                ones[j, t, :, 1:S + 1] = 1
    return [a.astype(np.float32) for a in (first, more, taps, ones.reshape(WJ, -1))]


def laid_out(i):
    w = np.zeros((P, NWTS), np.float32)

    def put(name, a, row=0, at=0):
        lo = WTS[name][0] + at
        w[row:row + a.shape[0], lo:lo + a.shape[1]] = a

    for b in range(NB):
        put("teT", i["L0_conv_w_te"].T, at=C * b)
    put("te", i["L0_conv_w_te"])
    for r in range(2):
        put("fc", i["L0_conv_w_fc"][H0 * r:H0 * r + H0], at=2 * H0 * r)
        put("fc2", i["L0_conv_w_fc"][0:H0], at=2 * H0 * r)
    copies = {"g1": 8, "b_fc": 2, "b_dw": 4, "ln2_scale": 2, "ln2_bias": 2, "ln1_scale": 8, "ln1_bias": 8}
    for n, v in enumerate(VECS):
        a = i[("L1_conv_" if v.startswith("ln") else "L0_conv_") + v]
        put("vecs", np.tile(a, copies.get(v, 1))[:, None], at=n)
    for q in range(4):
        put("tp", i["L0_conv_w_tp"], H0 * q, C * (q % 2))
        put("wfp", i["L0_conv_w_fp"], H0 * q, C * q)
    for h in range(2):
        put("wo", i["L1_conv_w_out"], CH * h, C * h)
    put("fe", i["L0_conv_w_fe"])
    put("bfe", i["L0_conv_b_fe"][None])
    for dy in range(3):
        for xx in range(NX):
            for dx in range(3):
                j = xx + dx
                for row, n in ((j * C, C), (WJ * C + j, 1)):
                    put("dw", np.broadcast_to(i["L0_conv_w_dw"][dy, dx], (n, H0)), row, H0 * (NX * dy + xx))
    put("b_tp", np.broadcast_to(i["L0_conv_b_tp"], (P, C)))
    put("b_fp", np.broadcast_to(i["L0_conv_b_fp"], (P, C)))
    for q in range(2):
        put("hid", i["L1_conv_w_hidden"][:, 96 * q:96 * q + 96].T, at=H0 * q)
    wq = i["L1_conv_w_qkv"].transpose(2, 1, 0, 3).reshape(2, HID // 2, TAPS * HID).transpose(1, 0, 2)
    return w, np.ascontiguousarray(wq)


def two_blocks(nc, x, weights, wqkv, first, more, taps, ones_rows, out):
    with ExitStack() as ctx:
        def sb(name, shape, dtype=F32):
            return ctx.enter_context(nc.sbuf_tensor(name, shape, dtype))

        def sem(name):
            return ctx.enter_context(nc.semaphore(name))

        bank = [ctx.enter_context(nc.psum_tensor(f"bank{i}", [P, 512], F32)) for i in range(8)]
        padded = nc.dram_tensor("padded", (SLOTS, C, NB, 8 * S2), F32, kind="Internal").ap()
        parts = nc.dram_tensor("parts", (NB, 8, 3, C, 8 * S2), BF16, kind="Internal").ap()

        kf, km, kt, wt = sb("kf", [P, NFIRST]), sb("km", [P, NMORE]), sb("kt", [C, NTAPC]), sb("wt", [P, NWTS])

        def const(name, rows=P):
            for place, k in ((FIRST, kf), (MORE, km), (TAPC, kt), (WTS, wt)):
                if name in place:
                    lo, hi = place[name]
                    return k[0:min(rows, k.shape[0]), lo:hi]

        def vec(name, rows=P):
            n = WTS["vecs"][0] + VECS.index(name)
            return wt[0:rows, n:n + 1]

        xt = sb("xt", [P, G2, S, C])
        x1 = sb("x1", [P, G2, S, C])
        x2 = sb("x2", [P, G2, S, C])
        xc = sb("xc", [P, G2, S, C])
        sq = sb("sq", [P, G2, S, C])
        zp = sb("zp", [P, G2, S2, C])
        st = sb("st", [P, G2, 4, S])
        spec = sb("spec", [P, 2 * UV])
        f1 = spec[:, 0:UV].rearrange("p (u b c) -> p u b c", u=U, b=NB)
        hc = spec[:, UV:2 * UV]
        tr = sb("tr", [P, G2, 2, 10, S2])
        UW = S * S2
        arena = sb("arena", [P, 4 * UW])
        sp = arena[:, 0:UV]
        gl = arena[:, 2176:2176 + 4096].rearrange("p (i b n) -> p i b n", i=2, b=NB)
        ht = arena[:, 6272:6272 + 4096].rearrange("p (u n) -> p u n", u=S)
        yy = arena[:, 10368:10368 + 4096].rearrange("p (j q r x) -> p j q r x", j=8, q=4, r=2)
        uw = arena[:, 0:NW * NB * S2].rearrange("p (t b y) -> p t b y", t=NW, b=NB)
        gd = arena[:, 4224:4224 + NW * NB * S].rearrange("p (t b y) -> p t b y", t=NW, b=NB)
        ui = arena[:, :].rearrange("p (i z n) -> p i z n", i=2, z=2)[:, :, 0, :].rearrange("p i (x t y) -> p i x t y", x=8, t=8)
        ui9 = arena[:, 3 * UW:4 * UW].bitcast(BF16).rearrange("p (i x t y) -> p i x t y", i=2, x=8, t=8)

        smix = sb("smix", [P, 2 * NB])
        wmix1 = sb("wmix1", [P, NB, 2, 2 * H0])
        hb = sb("hb", [H0, 2])
        wmix2 = sb("wmix2", [P, 2 * C])
        feg = sb("feg", [C, H0])
        brep = sb("brep", [C, KW])
        wdw = sb("wdw", [KW, 3, NX, H0])
        wq = sb("wq", [HID // 2, 2, TAPS, HID])
        wfold = x2[:, 0, :, :].rearrange("p x c -> p (x c)")[:, 0:2 * HID]
        w9 = sb("w9", [C, 2, HID])
        w9s = sb("w9s", [C, 3, HID], BF16)
        wc = sb("wc", [P, HID])
        wc9 = sb("wc9", [P, HID], BF16)
        tr9 = sb("tr9", [P, 2, 3, 10, S2], BF16)
        wo1 = sb("wo1", [P, 2 * C])
        wo2 = sb("wo2", [P, 2 * C])
        eps = sb("eps", [P, 2 + 10])
        tile = sb("tile", [P, 2, 4, P])
        tile9 = sb("tile9", [P, 2, 4, P], BF16)
        qk = sb("qk", [P, 2, 2, 4, CH])
        kh = sb("kh", [P, 2, 4, 3, SL])
        tp = sb("tp", [P, 2, 2, 4, 2, SL])
        pr = sb("pr", [P, 2, 4, 2, SL])
        prt = sb("prt", [P, 2, 2 * P])
        four = lambda a: a.rearrange("p (i k n) -> p i k n", i=2, k=4)
        vs, os_ = four(spec[:, 0:2048]), four(spec[:, UV:UV + 2048])
        oq = four(sq[:, :, :, :].rearrange("p g x c -> p (g x c)"))
        vo = four(zp[:, :, :, :].rearrange("p g x c -> p (g x c)")[:, 0:2048])
        stt = x1[:, :, :, :].rearrange("p g x c -> p (g x c)").rearrange("p (s n) -> p s n", s=8)
        ot = xt

        ld_x0, ld_x1, ld_first, ld_more, ld_taps, ld_w, ld_q, ld_ones = map(
            sem, "ld_x0 ld_x1 ld_first ld_more ld_taps ld_w ld_q ld_ones".split())
        ready0, zero9, tr_zero = sem("ready0"), sem("zero9"), sem("tr_zero")
        smix_done, te_mm, dw_w_mm, wc_mm, wfold_ready, w9_ready, w9_split, wc_ld = map(
            sem, "smix_done te_mm dw_w_mm wc_mm wfold_ready w9_ready w9_split wc_ld".split())
        fe_ready, mix_ready, wdw_ready, wo_ready = map(sem, "fe_ready mix_ready wdw_ready wo_ready".split())
        chain, act_chain, pool_chain = sem("chain"), sem("act_chain"), sem("pool_chain")
        centred, squared, var_sum, sd_done, z_done = map(sem, "centred squared var_sum sd_done z_done".split())
        f1_mm, f1_dve, f1_act, f2_mm, f2_ev = map(sem, "f1_mm f1_dve f1_act f2_mm f2_ev".split())
        m1_mm, gelu1, m2_mm, m2_ev, ht_mm, ht_ev = map(sem, "m1_mm gelu1 m2_mm m2_ev ht_mm ht_ev".split())
        i1_mm, i1_dve, i1_act, i2_mm, x1_done = map(sem, "i1_mm i1_dve i1_act i2_mm x1_done".split())
        xb_done, zp_zero, x1b_done, uw_zero = map(sem, "xb_done zp_zero x1b_done uw_zero".split())
        w_mm, w_act, w_dve = sem("w_mm"), sem("w_act"), sem("w_dve")
        dw_mm, gelu2, fp_mm, x2_done = sem("dw_mm"), sem("gelu2"), sem("fp_mm"), sem("x2_done")
        tr_mm, tr_ev = sem("tr_mm"), sem("tr_ev")
        st_dma = [sem(f"st_dma{g}") for g in range(G2)]
        st9_dma = [sem(f"st9_dma{b}") for b in range(NB)]
        part_act, part_dve = sem("part_act"), sem("part_dve")
        im_first, im_ld = sem("im_first"), [sem("im_ld0"), sem("im_ld1")]
        tiled, qk_mm, qk_ev, v_mm, v_ev = sem("tiled"), sem("qk_mm"), sem("qk_ev"), sem("v_mm"), sem("v_ev")
        f_mm, k_ev, prod, comb, p_mm, p_ev, o_mm, o_ev, osq, vo_done = map(
            sem, "f_mm k_ev prod comb p_mm p_ev o_mm o_ev osq vo_done".split())
        vo_last = sem("vo_last")
        s_mm, r_mm, r_act, r_var, r_sd, c_mm, ft_done, t_mm, out_add, out_st = map(
            sem, "s_mm r_mm r_act r_var r_sd c_mm ft_done t_mm out_add out_st".split())

        block = ctx.enter_context(nc.Block())

        def spans(n):
            return slice(512 * n, min(512 * n + 512, UV))

        def f1_bank(j):
            return bank[(0, 1, 2, 3, 4, 0, 1, 2)[j]]

        def f1_evac(copy, j):
            g, c4 = divmod(j, 4)
            src = f1_bank(j)[:, 0:4 * 2 * U].rearrange("p (c b u) -> p c b u", c=4, b=2)
            return copy(f1[:, :, 2 * g:2 * g + 2, 4 * c4:4 * c4 + 4].rearrange("p u b c -> p c b u"), src)

        def w_evac(copy, j):
            g, t4 = divmod(j, 4)
            src = bank[t4][0:WJ * C, :].rearrange("p (t b y) -> p t b y", t=4, b=2)
            return copy(uw[0:WJ * C, 4 * t4:4 * t4 + 4, 2 * g:2 * g + 2, 1:S + 1], src)

        def xs(h):
            return slice(S // 2 * h, S // 2 * (h + 1))

        def half_no(k, g, h):
            return 2 * (G2 * k + g) + h + 1

        def part_of(i, b2):
            return tr9[:, b2, i, 1:9, 1:S + 1]

        def left_of(g, b2):
            return xc[:, g].rearrange("p x c -> p (x c)").rearrange("p (b t y) -> p b t y", b=2, t=8)[:, b2]

        def tr_bank(g, i):
            return bank[(0, 6)[g] + i]

        def x1_bank(j):
            return bank[(4, 5, 2, 3)[j]]

        def unit_banks(u):
            return (bank[6], bank[7]) if u < 7 else (bank[0], bank[1])

        def token_bank(u, i):
            return bank[6 + i] if u < 7 else bank[3 + i]

        def gd_of(j):
            g, t4 = divmod(j, 4)
            return gd[:, 4 * t4:4 * t4 + 4, 2 * g:2 * g + 2, :]

        @block.sync
        def _(sp_):
            xin = x.rearrange("(g b) y x c -> g (b y) x c", g=G2)
            sp_.dma_start(xt[:, 0], xin[0]).then_inc(ld_x0, 16)
            sp_.dma_start(xt[:, 1], xin[1]).then_inc(ld_x1, 16)
            sp_.dma_start(km[:, :], more).then_inc(ld_more, 16)
            sp_.dma_start(wq[:, :, :, :].rearrange("p q t n -> p q (t n)"), wqkv).then_inc(ld_q, 16)
            sp_.wait_ge(wfold_ready, 1)
            for t in range(FULL):
                j, e = divmod(t, 2)
                sp_.dma_start(wc[C * t:C * t + C, :], wfold[32 * j:32 * j + C, HID * e:HID * e + HID]).then_inc(wc_ld, 16)
            sp_.wait_ge(w9_split, 1)
            for r, (_, part) in enumerate(SPLIT):
                sp_.dma_start(wc9[C * r:C * r + C, :], w9s[:, part, :]).then_inc(wc_ld, 16)
            sp_.wait_ge(m2_mm, 5)
            sp_.dma_start(uw[WJ * C:KW, :, :, :].rearrange("p t b y -> p (t b y)"), ones_rows).then_inc(ld_ones, 16)
            def store_padded(g):
                sp_.wait_ge(tr_ev, 2 * (g + 1))
                for s0, s1, lane, t0 in ((1, 9, 0, 1), (0, 1, 7, 0), (9, 10, 0, 2)):
                    sp_.dma_start(padded[s0:s1, :, 2 * g:2 * g + 2, :].rearrange("s c b n -> (s c) b n"),
                                  tr[C * lane:C * (lane + s1 - s0), g, :, t0:t0 + 8, :].rearrange("p b t y -> p b (t y)")).then_inc(st_dma[g], 16)

            def store_parts(b):
                sp_.wait_ge(part_dve, b + 3 + 2 * (b // 2))
                for s0, s1, lane, t0 in ((2, 9, 1, 1), (9, 10, 0, 2)):
                    for i in range(3):
                        sp_.dma_start(parts[b, s0 - 2:s1 - 2, i], tr9[C * lane:C * (lane + s1 - s0), b % 2, i, t0:t0 + 8, :]
                                      .rearrange("p t y -> p (t y)")).then_inc(st9_dma[b], 16)

            def load_taps(b, t0, t1, done):
                at, w = S2 * t0, S2 * (t1 - t0) - 2
                sp_.wait_ge(st_dma[b // 2], 16 * PAD_STORES)
                for t in range(FULL):
                    dx, dy = divmod(t, 3)
                    dst = ui[C * t:C * t + C, 1 - b % 2].rearrange("p x t y -> p x (t y)")
                    sp_.dma_start(dst[:, :, at:at + w], padded[dx:dx + 8, :, b, dy + at:dy + at + w].rearrange("s c n -> c s n")).then_inc(done, 16)

            def load_last(b, t0, t1, done):
                at, w = S2 * t0, S2 * (t1 - t0) - 2
                sp_.wait_ge(st9_dma[b], 16 * PART_STORES)
                rows = parts[b].rearrange("s i c n -> (i c) s n")
                for row, n in ((0, 3 * C), (3 * C, 3 * C), (6 * C, 2 * C)):
                    dst = ui9[row:row + n, 1 - b % 2].rearrange("p x t y -> p x (t y)")
                    sp_.dma_start(dst[:, :, at:at + w], rows[0:n, :, 2 + at:2 + at + w]).then_inc(done, 16)

            store_padded(0)
            store_parts(0)
            load_taps(0, 0, 4, im_first)
            load_last(0, 0, 4, im_first)
            load_taps(0, 4, 8, im_ld[0])
            load_last(0, 4, 8, im_ld[0])
            store_parts(1)
            sp_.wait_ge(fp_mm, 8)
            load_taps(1, 0, 8, im_ld[1])
            load_last(1, 0, 8, im_ld[1])
            store_padded(1)
            for b in (2, 3):
                store_parts(b)
                sp_.wait_ge(tiled, 8 * (b - 1))
                load_taps(b, 0, 8, im_ld[b % 2])
                load_last(b, 0, 8, im_ld[b % 2])
            ov = out.rearrange("(g b) y x c -> g (b y) x c", g=G2)
            for u in range(8):
                g, q = divmod(u, 4)
                sp_.wait_ge(out_add, u + 1)
                sp_.dma_start(ov[g, 32 * q:32 * q + 32], ot[32 * q:32 * q + 32, g]).then_inc(out_st, 16)
            sp_.wait_ge(out_st, 16 * 8)

        @block.gpsimd
        def _(pool):
            pool.memset(eps[:, 0:1], EPS0).then_inc(ready0, 1)
            pool.memset(eps[:, 1:2], EPS1).then_inc(ready0, 1)
            pool.memset(ht[:, U:S, :], 0.0).then_inc(ready0, 1)
            pool.memset(zp[:, :, 0:S2:S2 - 1, :], 0.0).then_inc(zp_zero, 1)
            pool.wait_ge(ld_first, 16)
            pool.wait_ge(ld_w, 16)
            pool.tensor_scalar(smix[:, :], const("mask"), vec("g1"), None, ALU.mult).then_inc(smix_done, 1)
            pool.memset(tr[:, :, :, :, :], 0.0).then_inc(tr_zero, 1)
            pool.memset(tr9[:, :, :, :, :], 0.0).then_inc(zero9, 1)

            def per_channel(name):
                return const(name).rearrange("p (a c) -> p a c", a=1).broadcast_to([P, S // 2, C])

            pool_links = [0]

            def pool_link(ins_):
                ins_.then_inc(pool_chain, 1)
                pool_links[0] += 1
                pool.wait_ge(pool_chain, pool_links[0])

            def split(left, a, part, signal):
                pool_link(pool.tensor_copy(part[0], a))
                pool_link(pool.tensor_tensor(left, a, part[0], ALU.subtract))
                pool_link(pool.tensor_copy(part[1], left))
                pool.tensor_tensor(part[2], left, part[1], ALU.subtract).then_inc(signal, 1)

            pool.wait_ge(w9_ready, 1)
            split(w9[:, 1, :], w9[:, 0, :], [w9s[:, i, :] for i in range(3)], w9_split)
            for g in range(G2):
                for h in range(2):
                    pool.wait_ge(centred, half_no(0, g, h))
                    pool.tensor_tensor(xt[:, g, xs(h)], xt[:, g, xs(h)], per_channel("b_tp"), ALU.add).then_inc(xb_done, 1)
            pool.wait_ge(m2_mm, 5)
            pool.memset(uw[0:WJ * C, :, :, 0:S2:S2 - 1], 0.0).then_inc(uw_zero, 1)
            for g in range(G2):
                for h in range(2):
                    pool.wait_ge(centred, half_no(1, g, h))
                    pool.tensor_tensor(x1[:, g, xs(h)], x1[:, g, xs(h)], per_channel("b_fp"), ALU.add).then_inc(x1b_done, 1)

            def times_v(m):
                u, k = divmod(m, 4)
                pool.wait_ge(o_ev, m + 1)
                if u >= 2:
                    pool.wait_ge(r_mm, u - 1)
                pool.tensor_tensor(vo[:, u % 2, k, :], vs[:, u % 2, k, :], os_[:, u % 2, k, :], ALU.mult).then_inc(vo_done, 1)

            for m in range(32):
                pool.wait_ge(prod, m + 1)
                if m >= 2:
                    pool.wait_ge(p_mm, m - 1)
                t, o = tp[:, m % 2], pr[:, m % 2]
                pool.tensor_tensor(o[:, :, 0, 0:NC], t[:, 0, :, 0, 0:NC], t[:, 0, :, 1, 0:NC], ALU.subtract)
                pool.tensor_tensor(o[:, :, 1, 0:NC], t[:, 1, :, 0, 0:NC], t[:, 1, :, 1, 0:NC], ALU.add)
                pool.tensor_copy(o[:, :, :, NC:SL], t[:, 0, :, :, NC:SL]).then_inc(comb, 1)
                if m >= 2:
                    times_v(m - 2)

        @block.scalar
        def _(act):
            act.dma_start(kf[:, :], first).then_inc(ld_first, 16)
            act.dma_start(wt[:, :], weights).then_inc(ld_w, 16)
            act.dma_start(kt[:, :], taps).then_inc(ld_taps, 16)

            tables = []

            def load_table(func):
                act.activation(eps[:, 2 + len(tables):3 + len(tables)], eps[:, 0:1], func)
                tables.append(func)

            def square(k, g, halves=(0, 1)):
                for h in halves:
                    act.wait_ge(centred, half_no(k, g, h))
                    act.activation(sq[:, g, xs(h)], xc[:, g, xs(h)], ACT.Square).then_inc(squared, 1)

            def deviation(k, g, halves=(0, 1)):
                for h in halves:
                    act.wait_ge(var_sum, half_no(k, g, h))
                    act.activation(st[:, g, 2, xs(h)], st[:, g, 1, xs(h)], ACT.Sqrt, bias=eps[:, k // 2:k // 2 + 1],
                                   scale=1.0 / C).then_inc(sd_done, 1)

            def part(g, i, b2):
                if i == 0:
                    act.wait_ge(zero9, 1)
                    act.wait_ge(tr_ev, 2 * g + 2)
                    if g == 1:
                        act.wait_ge(st9_dma[b2], 16 * PART_STORES)
                    act.copy(part_of(0, b2), tr[:, g, b2, 1:9, 1:S + 1]).then_inc(part_act, 1)
                else:
                    act.wait_ge(part_dve, 4 * g + b2 + 1)
                    act.copy(part_of(1, b2), left_of(g, b2)).then_inc(part_act, 1)

            act.wait_ge(ready0, 2)
            load_table(ACT.Sqrt)
            square(0, 0)
            deviation(0, 0)
            square(0, 1)
            deviation(0, 1)
            for j in (1, 3):
                act.wait_ge(f1_mm, j + 1)
                f1_evac(act.copy, j).then_inc(f1_act, 1)
            act.wait_ge(ld_w, 16)
            act.wait_ge(ld_taps, 16)
            act.activation(feg[:, :], const("fe", C), ACT.Copy, scale=vec("g2", C)).then_inc(fe_ready, 1)
            act.activation(brep[:, :], const("onessel", C), ACT.Copy, scale=vec("b2", C)).then_inc(fe_ready, 1)
            act.activation(wo1[:, :], const("wo"), ACT.Copy, scale=vec("ln2_scale")).then_inc(wo_ready, 1)
            act.activation(wo2[:, :], const("wo"), ACT.Copy, scale=vec("ln2_bias")).then_inc(wo_ready, 1)
            act.wait_ge(ld_first, 16)
            act.activation(wmix2[:, :], const("tp"), ACT.Copy, scale=const("sign")).then_inc(mix_ready, 1)
            act.wait_ge(smix_done, 1)
            act.wait_ge(te_mm, 1)
            for b in range(NB):
                for s in range(2):
                    act.activation(wmix1[:, b, s, :], bank[7][:, 0:2 * H0], ACT.Copy,
                                   scale=smix[:, NB * s + b:NB * s + b + 1]).then_inc(mix_ready, 1)
            act.activation(hb[:, 0:1], bank[7][0:H0, 64:65], ACT.Identity, bias=vec("b_te", H0)).then_inc(act_chain, 1)
            act.wait_ge(act_chain, 1)
            act.activation(hb[:, 1:2], hb[:, 0:1], ACT.Copy, scale=float(S * S)).then_inc(mix_ready, 1)
            for j in (5, 7):
                act.wait_ge(f1_mm, j + 1)
                f1_evac(act.copy, j).then_inc(f1_act, 1)
            act.wait_ge(wc_mm, 1)
            act.copy(w9[:, 0, :], bank[5][0:C, 0:HID]).then_inc(w9_ready, 1)
            act.copy(wfold[:, :], bank[6][:, 0:2 * HID]).then_inc(wfold_ready, 1)
            load_table(ACT.Gelu)
            for n in range(5):
                w = spans(n).stop - spans(n).start
                for b in range(NB):
                    act.wait_ge(m1_mm, NB * n + b + 1)
                    if n >= 2:
                        act.wait_ge(m2_mm, n - 1)
                    act.activation(gl[:, n % 2, b, 0:w], bank[4 + b][:, 0:w], ACT.Gelu, bias=vec("b_fc")).then_inc(gelu1, 1)
            load_table(ACT.Sqrt)
            for j in (1, 3, 4, 5, 6, 7):
                act.wait_ge(i1_mm, j + 1)
                act.copy(yy[:, j].rearrange("p q r x -> p (q r x)"), bank[j % 4][:, :]).then_inc(i1_act, 1)
                if j in (4, 5):
                    square(1, 0, (j - 4,))
                if j in (6, 7):
                    deviation(1, 0, (j - 6,))
            for j in range(4):
                act.wait_ge(w_mm, j + 1)
                if j == 0:
                    act.wait_ge(m2_mm, 5)
                w_evac(act.copy, j).then_inc(w_act, 1)
            for g in range(G2):
                load_table(ACT.Gelu)
                for j in range(4 * g, 4 * g + 4):
                    if j == 2:
                        load_table(ACT.Sqrt)
                        square(1, 1)
                        deviation(1, 1)
                        load_table(ACT.Gelu)
                    if j == 6:
                        part(0, 0, 0)
                        part(0, 0, 1)
                        part(0, 1, 0)
                    if j == 7:
                        part(0, 1, 1)
                    act.wait_ge(dw_mm, j + 1)
                    act.activation(gd_of(j), bank[4 + j % 4][:, :].rearrange("p (t b y) -> p t b y", t=4, b=2),
                                   ACT.Gelu, bias=vec("b_dw")).then_inc(gelu2, 1)
                load_table(ACT.Sqrt)
                square(2, g, (0,))
                if g == 0:
                    for j in (4, 5):
                        act.wait_ge(w_mm, j + 1)
                        w_evac(act.copy, j).then_inc(w_act, 1)
                square(2, g, (1,))
                deviation(2, g)

            for n in range(32 + 5):
                if n in (6, 7):
                    for b2 in range(2):
                        part(1, n - 6, b2)
                if n < 32:
                    u, k = divmod(n, 4)
                    act.wait_ge(qk_mm, n + 1)
                    if n >= 2:
                        act.wait_ge(f_mm, n - 1)
                    act.copy(qk[:, n % 2].rearrange("p r t c -> p t r c"),
                             bank[n % 2][:, :].rearrange("p (t r c) -> p t r c", t=4, r=2)).then_inc(qk_ev, 1)
                m = n - 3
                if 0 <= m < 32:
                    act.wait_ge(p_mm, m + 1)
                    if m >= 2:
                        act.wait_ge(o_mm, m - 1)
                    act.copy(prt[:, m % 2, :], bank[4][:, 0:2 * P]).then_inc(p_ev, 1)
                m = n - 1
                if 0 <= m < 32:
                    act.wait_ge(f_mm, m + 1)
                    if m >= 2:
                        act.wait_ge(prod, m - 1)
                    kf_ = bank[3][:, 256:512].rearrange("p (a r s) -> p a r s", a=4, r=2)
                    act.copy(kh[:, m % 2, :, 0:2, :], kf_)
                    act.copy(kh[:, m % 2, :, 2, :], kf_[:, :, 0, :]).then_inc(k_ev, 1)
                if n >= 8 and (n - 8) % 4 == 0 and (n - 8) // 4 < 8:
                    u = (n - 8) // 4
                    act.wait_ge(r_var, u + 1)
                    act.activation(stt[:, 3, :], stt[:, 2, :], ACT.Sqrt, bias=eps[:, 1:2]).then_inc(r_sd, 1)
                m = n - 3
                if 0 <= m < 32:
                    u, k = divmod(m, 4)
                    act.wait_ge(o_mm, m + 1)
                    if u >= 2:
                        act.wait_ge(r_mm, u - 1)
                        act.wait_ge(vo_done, 4 * u - 4)
                    act.copy(os_[:, u % 2, k, :], bank[5][:, 0:256]).then_inc(o_ev, 1)
                    act.wait_ge(o_ev, m + 1)
                    act.activation(oq[:, u % 2, k, :], os_[:, u % 2, k, :], ACT.Square).then_inc(osq, 1)
                if n < 32:
                    u, k = divmod(n, 4)
                    act.wait_ge(v_mm, n + 1)
                    if u >= 2:
                        act.wait_ge(c_mm, u - 1)
                        act.wait_ge(vo_done, 4 * u - 4)
                    act.copy(vs[:, u % 2, k, :], bank[2][:, 0:256]).then_inc(v_ev, 1)
                if n >= 7 and (n - 7) % 4 == 0 and (n - 7) // 4 < 8:
                    u = (n - 7) // 4
                    act.wait_ge(s_mm, u + 1)
                    if u >= 1:
                        act.wait_ge(ft_done, u)
                    act.copy(stt[:, 0, :], unit_banks(u)[0][:, 0:256])
                    act.activation(stt[:, 1, :], unit_banks(u)[0][:, 0:256], ACT.Square).then_inc(r_act, 1)

        @block.vector
        def _(dve):
            done = [0]

            def link(ins_):
                ins_.then_inc(chain, 1)
                done[0] += 1
                dve.wait_ge(chain, done[0])

            def bc(a):
                return a.rearrange("p (x a) -> p x a", a=1).broadcast_to([P, S // 2, C])

            def centre(g, h, src):
                link(dve.tensor_reduce(out=st[:, g, 0, xs(h)], in_=src[:, g, xs(h)], axis=AX.X, op=ALU.add))
                dve.scalar_tensor_tensor(out=xc[:, g, xs(h)], in0=bc(st[:, g, 0, xs(h)]), scalar=-1.0 / C, in1=src[:, g, xs(h)],
                                         op0=ALU.mult, op1=ALU.add).then_inc(centred, 1)

            def variance(k, g):
                for h in range(2):
                    dve.wait_ge(squared, half_no(k, g, h))
                    dve.tensor_reduce(out=st[:, g, 1, xs(h)], in_=sq[:, g, xs(h)], axis=AX.X, op=ALU.add).then_inc(var_sum, 1)

            def normalise(k, g, dst):
                for h in range(2):
                    dve.wait_ge(sd_done, half_no(k, g, h))
                    link(dve.reciprocal(st[:, g, 3, xs(h)], st[:, g, 2, xs(h)]))
                    dve.tensor_tensor(dst[:, xs(h)], xc[:, g, xs(h)], bc(st[:, g, 3, xs(h)]), ALU.mult).then_inc(z_done, 1)

            def split(g):
                dve.wait_ge(tr_mm, 2 * g + 2)
                for b2 in range(2):
                    dve.wait_ge(part_act, 4 * g + b2 + 1)
                    dve.tensor_tensor(left_of(g, b2), tr[:, g, b2, 1:9, 1:S + 1], part_of(0, b2), ALU.subtract).then_inc(part_dve, 1)
                for b2 in range(2):
                    dve.wait_ge(part_act, 4 * g + b2 + 3)
                    dve.tensor_tensor(part_of(2, b2), left_of(g, b2), part_of(1, b2), ALU.subtract).then_inc(part_dve, 1)

            def bordered(g):
                for i in range(2):
                    dve.wait_ge(tr_mm, 2 * g + i + 1)
                    dve.tensor_scalar(tr[:, g, :, 1 + 4 * i:5 + 4 * i, 1:S + 1], tr_bank(g, i)[:, :].rearrange("p (t b y) -> p b t y", t=4, b=2),
                                      vec("ln1_scale"), vec("ln1_bias"), ALU.mult, ALU.add).then_inc(tr_ev, 1)

            dve.wait_ge(ld_x0, 16)
            for h in range(2):
                centre(0, h, xt)
            variance(0, 0)
            dve.wait_ge(ld_x1, 16)
            centre(1, 0, xt)
            normalise(0, 0, sq[:, 0])
            centre(1, 1, xt)
            variance(0, 1)
            normalise(0, 1, sq[:, 1])
            for j in range(0, 8, 2):
                dve.wait_ge(f1_mm, j + 1)
                f1_evac(dve.tensor_copy, j).then_inc(f1_dve, 1)
            for n in range(5):
                dve.wait_ge(f2_mm, n + 1)
                dve.tensor_copy(sp[:, spans(n)], bank[n][:, 0:spans(n).stop - spans(n).start]).then_inc(f2_ev, 1)
            for n in range(6):
                if n < 5:
                    dve.wait_ge(m2_mm, n + 1)
                    dve.tensor_copy(hc[:, spans(n)], bank[n % 2][:, 0:spans(n).stop - spans(n).start]).then_inc(m2_ev, 1)
                if n >= 1:
                    m = n - 1
                    w = spans(m).stop - spans(m).start
                    dve.wait_ge(ht_mm, m + 1)
                    dve.tensor_copy(ht[:, 8 * m:8 * m + w // S, :].rearrange("p u n -> p (u n)"),
                                    bank[2 + m % 2][:, 0:w]).then_inc(ht_ev, 1)
            for j in (0, 2):
                dve.wait_ge(i1_mm, j + 1)
                dve.tensor_copy(yy[:, j].rearrange("p q r x -> p (q r x)"), bank[j][:, :]).then_inc(i1_dve, 1)
            dve.wait_ge(dw_w_mm, 1)
            dve.tensor_tensor(wdw[:, :, :, :].rearrange("p a b h -> p (a b) h"), const("dw", KW).rearrange("p (a h) -> p a h", h=H0),
                              bank[6][0:KW, 0:H0].rearrange("p (a h) -> p a h", a=1).broadcast_to([KW, 3 * NX, H0]), ALU.mult).then_inc(wdw_ready, 1)
            for g in range(G2):
                dve.wait_ge(xb_done, 2 * g + 2)
                for xh in range(2):
                    j = 2 * g + xh
                    cols = slice(32 * xh, 32 * xh + 32)
                    dve.wait_ge(i2_mm, j + 1)
                    o = dve.tensor_tensor(x1[:, g, cols, :], x1_bank(j)[:, :].rearrange("p (c x) -> p x c", c=C),
                                          xt[:, g, cols, :], ALU.add)
                    o.then_inc(x1_done, 1)
                    dve.wait_ge(x1_done, j + 1)
                    centre(g, xh, x1)
                if g == 0:
                    dve.wait_ge(zp_zero, 1)
                variance(1, g)
                normalise(1, g, zp[:, g, 1:S + 1])
            dve.wait_ge(wc_ld, 16 * (FULL + len(SPLIT)))
            for g in range(G2):
                for j in range(4 * g, 4 * g + 4):
                    t4 = j % 4
                    tx = lambda a: a[:, g, 16 * t4:16 * t4 + 16, :].rearrange("p (t x) c -> p t (x c)", t=4)
                    if t4 == 0:
                        dve.wait_ge(x1b_done, 2 * g + 1)
                    if t4 == 2:
                        dve.wait_ge(x1b_done, 2 * g + 2)
                    dve.wait_ge(fp_mm, j + 1)
                    dve.tensor_tensor(tx(x2), bank[j][:, 0:4 * FPN].rearrange("p (t n) -> p t n", t=4)[:, :, 0:NX * C],
                                      tx(x1), ALU.add).then_inc(x2_done, 1)
                    if j % 2 == 1:
                        dve.wait_ge(x2_done, j + 1)
                        centre(g, t4 // 2, x2)
                variance(2, g)
                normalise(2, g, xc[:, g])
                if g == 0:
                    for j in (6, 7):
                        dve.wait_ge(w_mm, j + 1)
                        w_evac(dve.tensor_copy, j).then_inc(w_dve, 1)
                    dve.wait_ge(tr_zero, 1)
                    bordered(0)
                    split(0)

            def gather(n):
                u, k = divmod(n, 4)
                b, yh = divmod(u, 2)
                if n == 0:
                    dve.wait_ge(im_first, 16 * (FULL + PART_LOADS))
                if n == 2 or n % 8 == 0 and n > 0:
                    dve.wait_ge(im_ld[b % 2], 16 * (FULL + PART_LOADS) * (b // 2 + 1))
                if n >= 2:
                    dve.wait_ge(v_mm, n - 1)
                for dst, src in ((tile, ui), (tile9, ui9)):
                    for h in range(2):
                        a = src[:, 1 - b % 2, :, 2 * k + h, 32 * yh:32 * yh + 32].rearrange("p x (t y) -> p t x y", t=2)
                        o = dve.tensor_copy(dst[:, n % 2, h::2].rearrange("p t (x y) -> p t x y", x=8), a)
                o.then_inc(tiled, 1)

            def add_result(u):
                g, q = divmod(u, 4)
                rows = slice(32 * q, 32 * q + 32)
                for i in range(2):
                    dve.wait_ge(t_mm, 2 * u + i + 1)
                    res = lambda a: a[rows, g].rearrange("p (k e) c -> p k e c", k=8)[:, :, 4 * i:4 * i + 4, :]
                    o = dve.tensor_tensor(res(ot), token_bank(u, i)[0:32, :].rearrange("p (e k c) -> p k e c", e=4, k=8),
                                          res(x2), ALU.add)
                o.then_inc(out_add, 1)

            gather(0)
            for n in range(32 + 7):
                if n == 7:
                    split(1)
                if n + 1 < 32:
                    gather(n + 1)
                if n == 0:
                    bordered(1)
                if n in (33, 34):
                    m = n - 3
                    dve.wait_ge(o_ev, m + 1)
                    dve.tensor_tensor(vo[:, 1, m % 4, :], vs[:, 1, m % 4, :], os_[:, 1, m % 4, :], ALU.mult).then_inc(vo_last, 1)
                m = n - 1
                if 0 <= m < 32:
                    dve.wait_ge(k_ev, m + 1)
                    if m >= 2:
                        dve.wait_ge(comb, m - 1)
                    for e in range(2):
                        o = dve.tensor_tensor(tp[:, m % 2, e].rearrange("p a r s -> p a (r s)"),
                                              bank[3][:, 0:256].rearrange("p (a n) -> p a n", a=4),
                                              kh[:, m % 2, :, e:e + 2, :].rearrange("p a r s -> p a (r s)"), ALU.mult)
                    o.then_inc(prod, 1)
                if n >= 8 and (n - 8) % 4 == 0 and (n - 8) // 4 < 8:
                    u = (n - 8) // 4
                    dve.wait_ge(r_sd, u + 1)
                    link(dve.reciprocal(stt[:, 5, :], stt[:, 3, :]))
                    link(dve.tensor_tensor(stt[:, 6, :], stt[:, 4, :], stt[:, 5, :], ALU.mult))
                if n >= 8 and (n - 8) % 4 == 0 and (n - 8) // 4 < 8:
                    u = (n - 8) // 4
                    dve.wait_ge(c_mm, u + 1)
                    txy = lambda a: a.rearrange("p (t x y) -> p t x y", t=2, x=8)
                    dve.tensor_tensor(stt[:, 7, :].rearrange("p (x t y) -> p t x y", t=2, x=8), txy(unit_banks(u)[0][:, 0:256]),
                                      txy(stt[:, 6, :]), ALU.add).then_inc(ft_done, 1)
                if n == 35:
                    add_result(6)
                if n >= 7 and (n - 7) % 4 == 0 and (n - 7) // 4 < 8:
                    u = (n - 7) // 4
                    dve.wait_ge(r_act, u + 1)
                    link(dve.tensor_tensor(stt[:, 2, :], unit_banks(u)[0][:, 256:512], stt[:, 1, :], ALU.subtract))
                    dve.tensor_scalar(stt[:, 2, :], stt[:, 2, :], 0.0, None, ALU.max).then_inc(r_var, 1)
                    dve.wait_ge(r_mm, u + 1)
                    link(dve.tensor_tensor(stt[:, 4, :], unit_banks(u)[1][:, 256:512], stt[:, 0, :], ALU.mult))
                    link(dve.tensor_tensor(stt[:, 4, :], unit_banks(u)[1][:, 0:256], stt[:, 4, :], ALU.subtract))
                if (n - 10) % 4 == 0 and (0 <= (n - 10) // 4 < 6 or n == 38):
                    add_result((n - 10) // 4)

        @block.tensor
        def _(pe):
            mm = pe.matmul
            def keep_warm(times, a, free=6, cols=512):
                for _ in range(times):
                    mm(bank[free][:, 0:cols], a[:, 0:P], a[:, 0:cols], start=True, stop=True)

            pe.wait_ge(ready0, 3)
            keep_warm(WARM, ht[:, U:U + 8, :].rearrange("p u n -> p (u n)"))
            pe.wait_ge(ld_w, 16)
            fc = const("fc", H0).rearrange("h (r n) -> h r n", r=2)
            for r in range(2):
                mm(bank[7][64 * r:64 * r + 64, 0:2 * H0], const("teT", H0), fc[:, r, :], start=True, stop=True)
            mm(bank[7][0:H0, 64:65], const("te", C), vec("b1", C), start=True, stop=True).then_inc(te_mm, 1)
            def depthwise_weights():
                pe.wait_ge(ld_taps, 16)
                pe.wait_ge(fe_ready, 2)
                mm(bank[6][0:KW, 0:H0], const("rep", C), feg[:, :], start=True, stop=False)
                mm(bank[6][0:KW, 0:H0], brep[:, :], const("fe", C), start=False, stop=False)
                mm(bank[6][0:KW, 0:H0], const("one1", 1), const("bfe", 1), start=False, stop=True).then_inc(dw_w_mm, 1)

            def conv_weights():
                pe.wait_ge(ld_q, 16)
                hid = const("hid", HID // 2).rearrange("p (q n) -> p q n", q=2)
                for j in range(4):
                    for q in range(2):
                        mm(bank[6][32 * j:32 * j + 32, 0:2 * HID], hid[:, q, :], wq[:, q, 2 * j:2 * j + 2, :].rearrange("p t n -> p (t n)"),
                           start=(q == 0), stop=(q == 1))
                for q in range(2):
                    last = mm(bank[5][0:32, 0:HID], hid[:, q, :], wq[:, q, FULL, :], start=(q == 0), stop=(q == 1))
                last.then_inc(wc_mm, 1)

            pe.wait_ge(ld_first, 16)
            for j in range(8):
                g, c4 = divmod(j, 4)
                if j == 4:
                    conv_weights()
                if j == 5:
                    pe.wait_ge(f1_dve, 1)
                if j == 6:
                    pe.wait_ge(f1_act, 1)
                if j == 7:
                    pe.wait_ge(f1_dve, 2)
                pe.wait_ge(z_done, half_no(0, g, 1))
                for c in range(4):
                    for r, name in enumerate(("f1c", "f1s")):
                        last = mm(f1_bank(j)[64 * r:64 * r + 64, 2 * U * c:2 * U * (c + 1)], sq[:, g, :, 4 * c4 + c], const(name),
                                  start=True, stop=True)
                last.then_inc(f1_mm, 1)
            pe.wait_ge(ld_more, 16)
            pe.wait_ge(f1_act, 4)
            pe.wait_ge(f1_dve, 4)
            for n in range(5):
                for u in range(8 * n, min(8 * n + 8, U)):
                    for r, name in enumerate(("dre", "dim")):
                        last = mm(bank[n][64 * r:64 * r + 64, S * (u % 8):S * (u % 8) + S],
                                  f1[:, u].rearrange("p b c -> p (b c)"), const(name), start=True, stop=True)
                last.then_inc(f2_mm, 1)

            def ht_step(m):
                pe.wait_ge(m2_ev, m + 1)
                if m >= 2:
                    pe.wait_ge(ht_ev, m - 1)
                for u in range(8 * m, min(8 * m + 8, U)):
                    for r, name in enumerate(("selre", "selim")):
                        last = mm(bank[2 + m % 2][64 * r:64 * r + 64, S * (u % 8):S * (u % 8) + S],
                                  hc[:, S * u:S * u + S], const(name), start=True, stop=True)
                last.then_inc(ht_mm, 1)

            def mix2(n):
                w = spans(n).stop - spans(n).start
                pe.wait_ge(gelu1, NB * n + NB)
                if n >= 2:
                    pe.wait_ge(m2_ev, n - 1)
                for b in range(NB):
                    last = mm(bank[n % 2][H0 * b:H0 * b + H0, 0:w], wmix2[:, :], gl[:, n % 2, b, 0:w], start=True, stop=True)
                last.then_inc(m2_mm, 1)

            pe.wait_ge(mix_ready, 10)
            pe.wait_ge(w9_ready, 1)
            pe.wait_ge(wfold_ready, 1)
            for n in range(5):
                w = spans(n).stop - spans(n).start
                pe.wait_ge(f2_ev, 5 if n == 0 else n + 1)
                for b in range(NB):
                    if n >= 1:
                        pe.wait_ge(gelu1, NB * (n - 1) + b + 1)
                    if n == 0:
                        mm(bank[4 + b][:, 0:1], const("fc2", H0), hb[:, 1:2], start=True, stop=True)
                    mm(bank[4 + b][:, 0:w], wmix1[:, b].rearrange("p s n -> p (s n)"), sp[:, spans(n)],
                       start=(n > 0), stop=True, skip_group_check=(n == 0)).then_inc(m1_mm, 1)
                if n >= 1:
                    mix2(n - 1)
                if n >= 2:
                    ht_step(n - 2)
            mix2(4)
            ht_step(3)
            ht_step(4)
            depthwise_weights()
            pe.wait_ge(ht_ev, 5)
            pe.wait_ge(ready0, 3)
            def inverse_x(g):
                for j in range(4 * g, 4 * g + 4):
                    for c in range(4):
                        for b2 in range(2):
                            last = mm(bank[j % 4][64 * b2:64 * b2 + 64, P * c:P * c + P], ht[:, :, C * (2 * g + b2) + 4 * (j % 4) + c],
                                      const("ev"), start=True, stop=True)
                    last.then_inc(i1_mm, 1)

            def inverse_y(g):
                pe.wait_ge(i1_dve, 2)
                pe.wait_ge(i1_act, 2 + 4 * g)
                if g == 1:
                    pe.wait_ge(w_act, 4)
                for j in range(2 * g, 2 * g + 2):
                    cols = slice(32 * (j % 2), 32 * (j % 2) + 32)
                    for r, name in enumerate(("e2re", "e2im")):
                        src = yy[:, 4 * g:4 * g + 4, :, r, cols].rearrange("p j q x -> p (j q) x")
                        last = mm(x1_bank(j)[:, :], const(name), src, start=(r == 0), stop=(r == 1))
                    last.then_inc(i2_mm, 1)

            inverse_x(0)
            inverse_y(0)
            inverse_x(1)
            pe.wait_ge(wdw_ready, 1)
            keep_warm(2, km)

            def windows(g):
                pe.wait_ge(z_done, half_no(1, g, 1))
                for t4 in range(4):
                    if g == 1:
                        pe.wait_ge(x2_done, t4 + 1)
                    for t in range(4):
                        x0 = NX * (4 * t4 + t)
                        last = pe.transpose(bank[t4][0:WJ * C, P * t:P * t + P], zp[:, g, x0:x0 + WJ, :].rearrange("p x c -> p (x c)"),
                                            const("ident"))
                    last.then_inc(w_mm, 1)

            def depthwise(j):
                g, t4 = divmod(j, 4)
                if g == 0:
                    pe.wait_ge(w_act, t4 + 1)
                    pe.wait_ge(x1_done, 2)
                    pe.wait_ge(wdw_ready, 1)
                else:
                    if t4 < 2:
                        pe.wait_ge(w_act, j + 1)
                    else:
                        pe.wait_ge(w_dve, t4 - 1)
                    pe.wait_ge(gelu2, j - 3)
                for dy in range(3):
                    last = mm(bank[4 + t4][:, :], wdw[:, dy].rearrange("p x h -> p (x h)"), uw[0:KW, 4 * t4:4 * t4 + 4, 2 * g:2 * g + 2, dy:dy + S],
                              start=(dy == 0), stop=(dy == 2))
                last.then_inc(dw_mm, 1)

            def project(j):
                g, t4 = divmod(j, 4)
                pe.wait_ge(gelu2, j + 1)
                if j in (2, 3):
                    pe.wait_ge(x1_done, j + 1)
                for t in range(4):
                    last = mm(bank[j][:, FPN * t:FPN * (t + 1)], gd[:, 4 * t4 + t, 2 * g:2 * g + 2, :].rearrange("p b y -> p (b y)"),
                              const("wfp"), start=True, stop=True)
                last.then_inc(fp_mm, 1)

            def channel_major(g):
                for i in range(2):
                    pe.wait_ge(z_done, half_no(2, g, i))
                    for t in range(4):
                        x0 = 8 * (4 * i + t)
                        last = pe.transpose(tr_bank(g, i)[:, P * t:P * t + P], xc[:, g, x0:x0 + 8, :].rearrange("p x c -> p (x c)"), const("ident"))
                    last.then_inc(tr_mm, 1)

            pe.wait_ge(i1_act, 6)
            windows(0)
            pe.wait_ge(uw_zero, 1)
            pe.wait_ge(ld_ones, 16)
            depthwise(0)
            depthwise(1)
            inverse_y(1)
            depthwise(2)
            project(0)
            depthwise(3)
            for j in range(1, 4):
                project(j)
            windows(1)
            depthwise(4)
            depthwise(5)
            channel_major(0)
            depthwise(6)
            project(4)
            depthwise(7)
            for j in range(5, 8):
                project(j)
            keep_warm(5, km, 2)
            pe.wait_ge(x2_done, 8)
            channel_major(1)
            keep_warm(1, km, 2)

            products = {"mean": (os_, const("mean"), 0, 0), "square": (oq, const("mean"), 0, 256), "B": (vs, wo1[:, :], 1, 256), "A": (vo, wo1[:, :], 1, 0)}

            def unit_products(which, u, ks):
                src, w, at, lo = products[which]
                dst = unit_banks(u)[at]
                for k in ks:
                    last = mm(dst[32 * k:32 * k + 32, lo:lo + 256], w, src[:, u % 2, k, :], start=True, stop=True)
                return last

            def to_tokens(u):
                pe.wait_ge(ft_done, u + 1)
                for e in range(8):
                    src = stt[:, 7, 32 * e:32 * e + 32]
                    last = pe.transpose(token_bank(u, e // 4)[0:32, P * (e % 4):P * (e % 4) + P], src, const("ident"))
                    if e % 4 == 3:
                        last.then_inc(t_mm, 1)

            pe.wait_ge(tr_ev, 2)
            pe.wait_ge(wo_ready, 2)
            pe.wait_ge(wc_ld, 16 * (FULL + len(SPLIT)))
            for n in range(32 + 5):
                if n < 32:
                    u, k = divmod(n, 4)
                    b, yh = divmod(u, 2)
                    pe.wait_ge(tiled, n + 1)
                    if n >= 2:
                        pe.wait_ge(qk_ev, n - 1)
                    for t in range(4):
                        mm(bank[n % 2][:, P * t:P * t + P], tile[:, n % 2, t, :], wc[:, 0:2 * CH], start=True, stop=False)
                        last = mm(bank[n % 2][:, P * t:P * t + P], tile9[:, n % 2, t, :], wc9[:, 0:2 * CH], start=False, stop=True)
                    last.then_inc(qk_mm, 1)
                    if n >= 1:
                        pe.wait_ge(v_ev, n)
                    for i, (w, a) in enumerate(((wc, tile), (wc9, tile9))):
                        for h in range(2):
                            last = mm(bank[2][64 * h:64 * h + 64, 0:256], w[:, 2 * CH:3 * CH], a[:, n % 2, h::2, :], start=(i == 0), stop=(i == 1))
                    last.then_inc(v_mm, 1)
                m = n - 3
                if 0 <= m < 32:
                    pe.wait_ge(comb, m + 1)
                    if m >= 1:
                        pe.wait_ge(p_ev, m)
                    for t in range(2):
                        src = pr[:, m % 2, 2 * t:2 * t + 2].rearrange("p a r s -> p (a r s)")
                        last = pe.transpose(bank[4][:, P * t:P * t + P], src, const("ident"))
                    last.then_inc(p_mm, 1)
                m = n - 1
                if 0 <= m < 32:
                    pe.wait_ge(qk_ev, m + 1)
                    if m >= 1:
                        pe.wait_ge(prod, m)
                    for r in range(2):
                        for t in range(2):
                            src = qk[:, m % 2, r, 2 * t:2 * t + 2, :].rearrange("p t c -> p (t c)")
                            last = mm(bank[3][:, 256 * r + P * t:256 * r + P * t + P], src, const("dq"), start=True, stop=True)
                    last.then_inc(f_mm, 1)
                if n == 34:
                    for which, ready in (("mean", o_ev), ("square", osq)):
                        pe.wait_ge(ready, 30)
                        unit_products(which, 7, range(2))
                m = n - 3
                if 0 <= m < 32:
                    pe.wait_ge(p_ev, m + 1)
                    if m >= 1:
                        pe.wait_ge(o_ev, m)
                    for t in range(2):
                        last = mm(bank[5][:, P * t:P * t + P], prt[:, m % 2, P * t:P * t + P], const("inv"), start=True, stop=True)
                    last.then_inc(o_mm, 1)
                if n >= 10 and (n - 10) % 4 == 0 and (n - 10) // 4 < 6:
                    to_tokens((n - 10) // 4)
                if n >= 7 and (n - 7) % 4 == 0 and (n - 7) // 4 < 7:
                    u = (n - 7) // 4
                    if u == 0:
                        pe.wait_ge(tr_ev, 4)
                    else:
                        pe.wait_ge(out_add, u)
                    pe.wait_ge(o_ev, 4 * u + 4)
                    unit_products("mean", u, range(4))
                    pe.wait_ge(osq, 4 * u + 4)
                    unit_products("square", u, range(4)).then_inc(s_mm, 1)
                    unit_products("B", u, range(4))
                    pe.wait_ge(vo_done, 4 * u + 4)
                    unit_products("A", u, range(4)).then_inc(r_mm, 1)
                if n == 32:
                    pe.wait_ge(qk_ev, 32)
                    pe.wait_ge(v_ev, 32)
                    unit_products("B", 7, range(4))
                if n == 34:
                    to_tokens(6)
                if n == 35:
                    for which, ready in (("mean", o_ev), ("square", osq)):
                        pe.wait_ge(ready, 32)
                        last = unit_products(which, 7, range(2, 4))
                    last.then_inc(s_mm, 1)
                    pe.wait_ge(vo_done, 30)
                    pe.wait_ge(vo_last, 2)
                    unit_products("A", 7, range(4)).then_inc(r_mm, 1)
                if n >= 8 and (n - 8) % 4 == 0 and (n - 8) // 4 < 8:
                    u = (n - 8) // 4
                    pe.wait_ge(r_var, u + 1)
                    for k in range(4):
                        last = mm(unit_banks(u)[0][32 * k:32 * k + 32, 0:256], wo2[:, :], vs[:, u % 2, k, :], start=True, stop=True)
                    last.then_inc(c_mm, 1)
            keep_warm(5, km, 2, 256)
            to_tokens(7)


_INS = ['x', 'L0_conv_g1', 'L0_conv_b1', 'L0_conv_g2', 'L0_conv_b2', 'L0_conv_w_te', 'L0_conv_b_te', 'L0_conv_w_fc',
        'L0_conv_b_fc', 'L0_conv_w_tp', 'L0_conv_b_tp', 'L0_conv_w_fe', 'L0_conv_b_fe', 'L0_conv_w_dw', 'L0_conv_b_dw',
        'L0_conv_w_fp', 'L0_conv_b_fp', 'L1_conv_w_hidden', 'L1_conv_w_qkv', 'L1_conv_w_out', 'L1_conv_ln1_scale',
        'L1_conv_ln1_bias', 'L1_conv_ln2_scale', 'L1_conv_ln2_bias']


def kernel(**inputs):
    import concourse.bacc as _bacc
    from concourse.bass_utils import run_bass_kernel_spmd as _run

    nc = _bacc.Bacc("TRN2", target_bir_lowering=False, num_devices=1)
    given = {name: np.asarray(inputs[name]) for name in _INS}
    w, wq = laid_out(given)
    first, more, taps, ones = constants()
    arrays = {"x": np.ascontiguousarray(given["x"]), "weights": w, "w_qkv": wq, "first": first, "more": more, "taps": taps, "ones_rows": ones}
    args = [nc.dram_tensor(name, a.shape, F32, kind="ExternalInput").ap() for name, a in arrays.items()]
    out = nc.dram_tensor("out", (NB, S, S, C), F32, kind="ExternalOutput").ap()
    two_blocks(nc, *args, out)
    r = _run(nc, [arrays], core_ids=[0])
    return r.results[0]["out"]
```
